# Optimizing a Trainium2 kernel written in Bass

```python
import numpy as np
import jax
import jax.numpy as jnp

def _softmax(x, axis=-1):
    return jax.nn.softmax(x, axis=axis)

def _gelu(x):
    return jax.nn.gelu(x, approximate=True)

def _silu(x):
    return jax.nn.silu(x)

def _sigmoid(x):
    return jax.nn.sigmoid(x)

def _layernorm(x, axis=-1, eps=1e-05):
    m = jnp.mean(x, axis=axis, keepdims=True)
    v = jnp.var(x, axis=axis, keepdims=True)
    return (x - m) / jnp.sqrt(v + eps)

def _scatter_add(tgt, idx, src, axis=0):
    return tgt.at[idx].add(src)

def _segment_sum(src, seg, n):
    return jax.ops.segment_sum(src, seg, n)
kernel_name = 'mk_xattn_ffn_d2_seqx_r2_b8a53c'

def setup_inputs(seed: int=0):
    np.random.seed(seed)
    _w = jnp.asarray

    def _rec_inputs():
        import jax
        import jax.numpy as jnp
        _rk = jax.random.key(seed)
        x = -0.0002928 + 1 * jax.random.normal(jax.random.fold_in(_rk, 1), (16, 100, 512), jnp.float32)
        _lenS = 100 - jax.random.randint(jax.random.fold_in(_rk, 7), (16,), 0, max(1, 100 // 4) + 1, jnp.int32)
        _lenS2 = 722 - jax.random.randint(jax.random.fold_in(_rk, 8), (16,), 0, max(1, 722 // 4) + 1, jnp.int32)
        _ctx_1024P = jax.random.normal(jax.random.fold_in(_rk, 11), (16, 16, 512), jnp.float32)
        _ctx_1024c = jax.random.dirichlet(jax.random.fold_in(_rk, 511), 0.3 * jnp.ones((16,), jnp.float32), (16, 722))
        _ctx_1024t = jnp.einsum('bsk,bkd->bsd', _ctx_1024c, _ctx_1024P)
        _ctx_1024t = _ctx_1024t * jax.lax.rsqrt(jnp.mean(jnp.square(_ctx_1024t)) + 1e-12) * 0.953939
        ctx_1024 = -1.39393e-06 + 0.999914 * (_ctx_1024t + 0.3 * jax.random.normal(jax.random.fold_in(_rk, 611), (16, 722, 512), jnp.float32))
        return (x, ctx_1024)
    x, ctx_1024 = _rec_inputs()

    def _L0_xattn_setup():
        import jax, jax.numpy as jnp
        import numpy as np
        D_MODEL, D_K, D_V, H = (512, 64, 64, 16)
        key = jax.random.key(seed)
        ks = jax.random.split(key, 11)
        b, nq, nk = (2, 1024, 1024)
        queries = jax.random.normal(ks[0], (b, nq, D_MODEL), dtype=jnp.float32)
        keys = jax.random.normal(ks[1], (b, nk, D_MODEL), dtype=jnp.float32)
        values = jax.random.normal(ks[2], (b, nk, D_MODEL), dtype=jnp.float32)

        def xavier(k, shape):
            fan_in, fan_out = (shape[1], shape[0])
            lim = np.sqrt(6.0 / (fan_in + fan_out)).astype(np.float32)
            return jax.random.uniform(k, shape, jnp.float32, -lim, lim)
        Wq = xavier(ks[3], (H * D_K, D_MODEL))
        bq = jnp.zeros((H * D_K,), jnp.float32)
        Wk = xavier(ks[4], (H * D_K, D_MODEL))
        bk = jnp.zeros((H * D_K,), jnp.float32)
        Wv = xavier(ks[5], (H * D_V, D_MODEL))
        bv = jnp.zeros((H * D_V,), jnp.float32)
        Wo = xavier(ks[6], (D_MODEL, H * D_V))
        bo = jnp.zeros((D_MODEL,), jnp.float32)
        return {'queries': queries, 'keys': keys, 'values': values, 'Wq': Wq, 'bq': bq, 'Wk': Wk, 'bk': bk, 'Wv': Wv, 'bv': bv, 'Wo': Wo, 'bo': bo}
    _L0_xattn_all = _L0_xattn_setup()
    _L0_xattn_in = {k: v for k, v in _L0_xattn_all.items() if k in ('Wq', 'bq', 'Wk', 'bk', 'Wv', 'bv', 'Wo', 'bo')}
    del _L0_xattn_all

    def _L0_ffn_setup():
        import jax, jax.numpy as jnp
        import numpy as np
        B, L, H, E, FF, C = (4, 1024, 512, 8, 2048, 2)
        key = jax.random.key(seed)
        ks = jax.random.split(key, 6)
        s = 0.02
        return {'x': jax.random.normal(ks[0], (B, L, H), dtype=jnp.float32), 'Wg': jax.random.normal(ks[1], (H, E), dtype=jnp.float32) * s, 'W1': jax.random.normal(ks[2], (E, H, FF), dtype=jnp.float32) * s, 'b1': jnp.zeros((E, FF), dtype=jnp.float32), 'W2': jax.random.normal(ks[3], (E, FF, H), dtype=jnp.float32) * s, 'b2': jnp.zeros((E, H), dtype=jnp.float32)}
    _L0_ffn_all = _L0_ffn_setup()
    _L0_ffn_in = {k: v for k, v in _L0_ffn_all.items() if k in ('Wg', 'W1', 'b1', 'W2', 'b2')}
    del _L0_ffn_all

    def _L1_xattn_setup():
        import jax, jax.numpy as jnp
        import numpy as np
        EMBED_DIM = 512
        NUM_HEAD = 16
        HEAD_DIM = EMBED_DIM // NUM_HEAD
        SCALE = HEAD_DIM ** (-0.5)
        key = jax.random.key(seed)
        ks = jax.random.split(key, 8)
        B, N, K, D = (2, 1024, 1024, EMBED_DIM)
        s = D ** (-0.5)
        return {'x': jax.random.normal(ks[0], (B, N, D), jnp.float32), 'ctx': jax.random.normal(ks[1], (B, K, D), jnp.float32), 'Wq': jax.random.normal(ks[2], (D, D), jnp.float32) * s, 'bq': jnp.zeros((D,), jnp.float32), 'Wkv': jax.random.normal(ks[3], (D, 2 * D), jnp.float32) * s, 'bkv': jnp.zeros((2 * D,), jnp.float32), 'Wproj': jax.random.normal(ks[4], (D, D), jnp.float32) * s, 'bproj': jnp.zeros((D,), jnp.float32)}
    _L1_xattn_all = _L1_xattn_setup()
    _L1_xattn_in = {k: v for k, v in _L1_xattn_all.items() if k in ('Wq', 'bq', 'Wkv', 'bkv', 'Wproj', 'bproj')}
    del _L1_xattn_all

    def _L1_ffn_setup():
        import jax, jax.numpy as jnp
        import numpy as np
        key = jax.random.key(seed)
        ks = jax.random.split(key, 5)
        B, T, D, E = (4, 1024, 512, 8)
        inputs = jax.random.normal(ks[0], (B, T, D), dtype=jnp.float32)
        Wr = jax.random.normal(ks[1], (D, E), dtype=jnp.float32) * 0.02
        br = jnp.zeros((E,), dtype=jnp.float32)
        W1 = jax.random.normal(ks[2], (E, D, D), dtype=jnp.float32) * 0.02
        b1 = jnp.zeros((E, D), dtype=jnp.float32)
        W2 = jax.random.normal(ks[3], (E, D, D), dtype=jnp.float32) * 0.02
        b2 = jnp.zeros((E, D), dtype=jnp.float32)
        return {'inputs': inputs, 'Wr': Wr, 'br': br, 'W1': W1, 'b1': b1, 'W2': W2, 'b2': b2}
    _L1_ffn_all = _L1_ffn_setup()
    _L1_ffn_in = {k: v for k, v in _L1_ffn_all.items() if k in ('Wr', 'br', 'W1', 'b1', 'W2', 'b2')}
    del _L1_ffn_all
    return {'x': x, 'ctx_1024': ctx_1024, 'L0_xattn_Wq': _L0_xattn_in['Wq'], 'L0_xattn_bq': _L0_xattn_in['bq'], 'L0_xattn_Wk': _L0_xattn_in['Wk'], 'L0_xattn_bk': _L0_xattn_in['bk'], 'L0_xattn_Wv': _L0_xattn_in['Wv'], 'L0_xattn_bv': _L0_xattn_in['bv'], 'L0_xattn_Wo': _L0_xattn_in['Wo'], 'L0_xattn_bo': _L0_xattn_in['bo'], 'L0_ffn_Wg': _L0_ffn_in['Wg'], 'L0_ffn_W1': _L0_ffn_in['W1'], 'L0_ffn_b1': _L0_ffn_in['b1'], 'L0_ffn_W2': _L0_ffn_in['W2'], 'L0_ffn_b2': _L0_ffn_in['b2'], 'L1_xattn_Wq': _L1_xattn_in['Wq'], 'L1_xattn_bq': _L1_xattn_in['bq'], 'L1_xattn_Wkv': _L1_xattn_in['Wkv'], 'L1_xattn_bkv': _L1_xattn_in['bkv'], 'L1_xattn_Wproj': _L1_xattn_in['Wproj'], 'L1_xattn_bproj': _L1_xattn_in['bproj'], 'L1_ffn_Wr': _L1_ffn_in['Wr'], 'L1_ffn_br': _L1_ffn_in['br'], 'L1_ffn_W1': _L1_ffn_in['W1'], 'L1_ffn_b1': _L1_ffn_in['b1'], 'L1_ffn_W2': _L1_ffn_in['W2'], 'L1_ffn_b2': _L1_ffn_in['b2']}

def reference(x, ctx_1024, L0_xattn_Wq, L0_xattn_bq, L0_xattn_Wk, L0_xattn_bk, L0_xattn_Wv, L0_xattn_bv, L0_xattn_Wo, L0_xattn_bo, L0_ffn_Wg, L0_ffn_W1, L0_ffn_b1, L0_ffn_W2, L0_ffn_b2, L1_xattn_Wq, L1_xattn_bq, L1_xattn_Wkv, L1_xattn_bkv, L1_xattn_Wproj, L1_xattn_bproj, L1_ffn_Wr, L1_ffn_br, L1_ffn_W1, L1_ffn_b1, L1_ffn_W2, L1_ffn_b2):
    import jax
    import jax.numpy as jnp

    def _L0_xattn_ref(queries, keys, values, Wq, bq, Wk, bk, Wv, bv, Wo, bo):
        import jax, jax.numpy as jnp
        import numpy as np
        D_MODEL, D_K, D_V, H = (512, 64, 64, 16)
        b, nq, _ = queries.shape
        nk = keys.shape[1]
        scale = 1.0 / np.sqrt(D_K).astype(np.float32)
        q = (queries @ Wq.T + bq).reshape(b, nq, H, D_K).transpose(0, 2, 1, 3)
        k = (keys @ Wk.T + bk).reshape(b, nk, H, D_K).transpose(0, 2, 1, 3)
        v = (values @ Wv.T + bv).reshape(b, nk, H, D_V).transpose(0, 2, 1, 3)
        att = jnp.einsum('bhqd,bhkd->bhqk', q, k) * scale
        att = jax.nn.softmax(att, axis=-1)
        out = jnp.einsum('bhqk,bhkd->bhqd', att, v)
        out = out.transpose(0, 2, 1, 3).reshape(b, nq, H * D_V)
        return out @ Wo.T + bo

    def _L0_ffn_ref(x, Wg, W1, b1, W2, b2):
        import jax, jax.numpy as jnp
        import numpy as np
        B, L, H, E, FF, C = (4, 1024, 512, 8, 2048, 2)
        b, l, h = x.shape
        e = Wg.shape[1]
        n = b * l
        k = min(max(int(n * C / e), 1), n)
        xt = x.reshape(n, h)
        S = jax.nn.sigmoid(xt @ Wg).T
        G, I = jax.lax.top_k(S, k)
        ex = xt[I]
        hid = jax.nn.gelu(jnp.einsum('ekh,ehf->ekf', ex, W1) + b1[:, None, :], approximate=False)
        out = (jnp.einsum('ekf,efh->ekh', hid, W2) + b2[:, None, :]) * G[..., None]
        new_x = jnp.zeros_like(xt).at[I.reshape(-1)].add(out.reshape(-1, h))
        return new_x.reshape(b, l, h)

    def _L1_xattn_ref(x, ctx, Wq, bq, Wkv, bkv, Wproj, bproj):
        import jax, jax.numpy as jnp
        import numpy as np
        EMBED_DIM = 512
        NUM_HEAD = 16
        HEAD_DIM = EMBED_DIM // NUM_HEAD
        SCALE = HEAD_DIM ** (-0.5)
        B, N, D = x.shape
        K = ctx.shape[1]
        H, hd = (NUM_HEAD, HEAD_DIM)
        q = (x @ Wq + bq).reshape(B, N, H, hd).transpose(0, 2, 1, 3)
        kv = (ctx @ Wkv + bkv).reshape(B, K, 2, H, hd).transpose(2, 0, 3, 1, 4)
        k, v = (kv[0], kv[1])
        attn = jnp.einsum('bhnd,bhkd->bhnk', q * SCALE, k)
        attn = jax.nn.softmax(attn, axis=-1)
        out = jnp.einsum('bhnk,bhkd->bhnd', attn, v)
        out = out.transpose(0, 2, 1, 3).reshape(B, N, D)
        return out @ Wproj + bproj

    def _L1_ffn_ref(inputs, Wr, br, W1, b1, W2, b2):
        import jax, jax.numpy as jnp
        import numpy as np
        B, T, D = inputs.shape
        E = Wr.shape[1]
        x = inputs.reshape(B * T, D)
        N = x.shape[0]
        C = N // E
        logits = x @ Wr + br
        probs = jax.nn.softmax(logits, axis=-1)
        gate = jnp.max(probs, axis=-1, keepdims=True)
        idx = jnp.argmax(probs, axis=-1)
        mask = jax.nn.one_hot(idx, E, dtype=jnp.float32)
        pos = (jnp.cumsum(mask, axis=0) * mask).astype(jnp.int32)
        mask = mask * (pos < C).astype(jnp.float32)
        mask_flat = jnp.sum(mask, axis=-1, keepdims=True)
        gate = gate * mask_flat
        combine = (gate * mask_flat * jax.nn.one_hot(idx, E, dtype=jnp.float32))[..., None] * jax.nn.one_hot(pos, C, dtype=jnp.float32)
        dispatch = combine
        expert_in = jnp.einsum('nd,nec->ecd', x, dispatch)
        h = jax.nn.relu(jnp.einsum('ecd,edf->ecf', expert_in, W1) + b1[:, None, :])
        eo = jnp.einsum('ecf,efd->ecd', h, W2) + b2[:, None, :]
        out = jnp.einsum('ecd,nec->nd', eo, combine)
        return out.reshape(B, T, D)
    x = x + _L0_xattn_ref(_layernorm(x, axis=-1), ctx_1024, ctx_1024, L0_xattn_Wq, L0_xattn_bq, L0_xattn_Wk, L0_xattn_bk, L0_xattn_Wv, L0_xattn_bv, L0_xattn_Wo, L0_xattn_bo)
    x = x + _L0_ffn_ref(_layernorm(x, axis=-1), L0_ffn_Wg, L0_ffn_W1, L0_ffn_b1, L0_ffn_W2, L0_ffn_b2)
    x = x + _L1_xattn_ref(_layernorm(x, axis=-1), ctx_1024, L1_xattn_Wq, L1_xattn_bq, L1_xattn_Wkv, L1_xattn_bkv, L1_xattn_Wproj, L1_xattn_bproj)
    x = x + _L1_ffn_ref(_layernorm(x, axis=-1), L1_ffn_Wr, L1_ffn_br, L1_ffn_W1, L1_ffn_b1, L1_ffn_W2, L1_ffn_b2)
    return x

_drawn_inputs = setup_inputs


def setup_inputs(seed=0):
    import zlib

    import numpy as np

    out = dict(_drawn_inputs(seed))
    spreads = {'L0_xattn_bq': (0.0, 0.336),
     'L0_xattn_bk': (0.0, 0.8),
     'L0_xattn_bv': (0.0, 0.1),
     'L0_xattn_bo': (0.0, 0.1),
     'L0_ffn_b1': (0.0, 0.1),
     'L0_ffn_b2': (0.0, 0.1),
     'L1_xattn_bq': (0.0, 0.474),
     'L1_xattn_bkv': (0.0, 0.1),
     'L1_xattn_bproj': (0.0, 0.1),
     'L1_ffn_br': (0.0, 0.747),
     'L1_ffn_b1': (0.0, 0.8),
     'L1_ffn_b2': (0.0, 0.475)}
    factors = {'L1_ffn_Wr': 3.306, 'L1_ffn_W1': 8.0, 'L1_ffn_W2': 6.908}
    for name, (base, spread) in spreads.items():
        noise = np.random.default_rng([zlib.crc32(name.encode()), seed]).standard_normal(out[name].shape)
        drawn = base * np.exp(spread * noise) if base else spread * noise
        out[name] = jnp.asarray(drawn.astype(out[name].dtype))
    for name, factor in factors.items():
        out[name] = (out[name] * factor).astype(out[name].dtype)
    return out
```

```python
from contextlib import ExitStack

import concourse.bass as bass
from concourse import mybir
import numpy as np

F32 = mybir.dt.float32
F32R = mybir.dt.float32r
F16 = mybir.dt.float16
BF16 = mybir.dt.bfloat16
I32 = mybir.dt.int32
U32 = mybir.dt.uint32
ALU = mybir.AluOpType
ACT = mybir.ActivationFunctionType
AX_X = mybir.AxisListType.X

P = 128
NB = 16
NQ = 100
NT = NB * NQ
NK = 722
D = 512
DC = D // P
KT = 6
KR = 121
NKP = KT * KR
KA = 362
KH = NK // 2
KPAD = 724
TW = 512
TT = TW // P
E = 8
REP = P // E
EPS = 1e-5
SLOT_MAX = 200
ROWS = NT + SLOT_MAX
TABLE_W = D + E


def f32(ap):
    return ap.bitcast(F32)


def three_passes(hi_lo_w, hi_lo_m):
    (w_hi, w_lo), (m_hi, m_lo) = hi_lo_w, hi_lo_m
    return [(w_lo, m_hi), (w_hi, m_lo), (w_hi, m_hi)]


def product(nc, out, chunks, first=True, final=True):
    todo = [p for c in chunks for p in three_passes(*c)]
    for n, (w, m) in enumerate(todo):
        last = nc.tensor.matmul(out, w, m, start=(first and n == 0), stop=(final and n == len(todo) - 1))
    return last


class Chain:

    def __init__(self, eng, sem, start=0):
        self.eng, self.sem, self.start, self.n = eng, sem, start, 0

    def step(self, ins):
        self.n += 1
        ins.then_inc(self.sem, 1)

    def wait(self):
        self.eng.wait_ge(self.sem, self.start + self.n)

    def link(self, ins):
        self.step(ins)
        self.wait()


def wait_first(eng, sem, value, passed):
    eng.wait_ge(sem, value)
    eng.sem_inc(passed, 1)


class Stage:

    def __init__(self, nc, ctx, tag):
        self.nc, self.ctx, self.tag = nc, ctx, tag
        self.sems = []
        ctx.callback(self.clear)

    def clear(self):
        if self.sems:
            self.nc.clear_and_free_semaphores(self.sems)
            self.nc.all_engine_barrier()

    def sb(self, name, shape, dt):
        return self.ctx.enter_context(self.nc.sbuf_tensor(f"{self.tag}_{name}", shape, dt))

    def ps(self, name, shape, dt=F32):
        return self.ctx.enter_context(self.nc.psum_tensor(f"{self.tag}_{name}", shape, dt))

    def sem(self, name):
        self.sems.append(self.nc.alloc_semaphore(f"{self.tag}_{name}"))
        return self.sems[-1]


def layernorm_stats(nc, dve, chain, x_all, bufs, var_ready, std_ready):
    stats, moments, veps, std, rstd, tmp = bufs
    for b in range(NB):
        ins = nc.vector.bn_stats(stats[:, b, :], x_all[:, b, :])
    chain.link(ins)
    for b in range(NB):
        ins = nc.vector.bn_aggr(moments[:, b, :], stats[:, b, :])
    chain.link(ins)
    nc.vector.tensor_scalar(veps[:], moments[:, :, 1], EPS, None, ALU.add).then_inc(var_ready, 1)
    dve.wait_ge(std_ready, 1)
    chain.link(nc.vector.reciprocal(rstd[:], std[:]))
    chain.link(nc.vector.tensor_tensor(tmp[:], rstd[:], rstd[:], ALU.mult))
    chain.link(nc.vector.tensor_tensor(tmp[:], tmp[:], veps[:], ALU.mult))
    chain.link(nc.vector.tensor_scalar(tmp[:], tmp[:], -0.5, 1.5, ALU.mult, ALU.add))
    chain.link(nc.vector.tensor_tensor(rstd[:], rstd[:], tmp[:], ALU.mult))


def layernorm_buffers(st):
    return (st.sb("stats", [NQ, NB, 6], F32), st.sb("moments", [NQ, NB, 2], F32), st.sb("veps", [NQ, NB], F32),
            st.sb("std", [NQ, NB], F32), st.sb("rstd", [NQ, NB], F32), st.sb("newton", [NQ, NB], F32))


def setup_stage(nc, ident):
    with ExitStack() as ctx:
        st = Stage(nc, ctx, "setup")
        zeroed = st.sem("zeroed")
        made = st.sem("made")
        with nc.Block() as block:
            @block.gpsimd
            def _(pool):
                nc.gpsimd.memset(ident[:], 0.0).then_inc(zeroed, 1)
                pool.wait_ge(zeroed, 1)
                nc.gpsimd.affine_select(out=ident[:], in_=ident[:], compare_op=ALU.not_equal, fill=1.0, base=0,
                                        pattern=[[-1, P]], channel_multiplier=1).then_inc(made, 1)
                pool.wait_ge(made, 1)


def query_stage(nc, tag, ident, x_rows, wq_t, bq_cols, scale, queries):
    T = wq_t.shape[1] // P
    CG = 4
    NG = NB // CG
    with ExitStack() as ctx:
        st = Stage(nc, ctx, tag)
        x_all = st.sb("x", [NQ, NB, D], F32)
        ln = layernorm_buffers(st)
        stats, moments, veps, std, rstd, _ = ln
        xt_hi = st.sb("xt_hi", [P, DC, NT], F32R)
        xt_lo = st.sb("xt_lo", [P, DC, NT], F32R)
        w_raw = st.sb("w_raw", [P, DC, T * P], F32)
        w_hi = st.sb("w_hi", [P, DC, T * P], F32R)
        w_lo = st.sb("w_lo", [P, DC, T * P], F32R)
        bias = st.sb("bias", [P, T], F32)
        bias_s = st.sb("bias_s", [P, T], F32)
        q_val = st.sb("q_val", [P, 2, CG * NQ], F32)
        q_out = st.sb("q_out", [P, 2, CG, 2, NQ], F32R)
        xp = [st.ps(f"xp{i}", [P, DC, P]) for i in range(2)]
        qp = [st.ps(f"qp{i}", [P, CG * NQ]) for i in range(4)]

        x_in, w_in, b_in = st.sem("x_in"), st.sem("w_in"), st.sem("b_in")
        var_ready, std_ready, step = st.sem("var_ready"), st.sem("std_ready"), st.sem("step")
        xn_ready, xt_done, xt_hi_done, xt_lo_done = (st.sem(n) for n in ("xn_ready", "xt_done", "xt_hi_done", "xt_lo_done"))
        w_hi_done, w_lo_done, bias_done = st.sem("w_hi_done"), st.sem("w_lo_done"), st.sem("bias_done")
        q_done, q_val_done, q_hi_done, q_lo_done = (st.sem(n) for n in ("q_done", "q_val_done", "q_hi_done", "q_lo_done"))
        q_stored = [st.sem(f"q_stored{i}") for i in range(2)]

        with nc.Block() as block:
            @block.sync
            def _(sp):
                sp.dma_start(x_all[:], x_rows.rearrange("(b p) d -> p b d", p=NQ)).then_inc(x_in, 16)
                sp.dma_start(w_raw[:], wq_t.rearrange("(c p) n -> p c n", p=P)).then_inc(w_in, 16)
                sp.dma_start(bias[:], bq_cols).then_inc(b_in, 16)
                with sp.Fori(0, NG) as g:
                    for t in range(T):
                        sp.wait_ge(q_lo_done, g * T + t + 1)
                        sp.dma_start(queries[:, bass.ds(g * CG, CG), t], f32(q_out[:, t % 2])).then_inc(q_stored[t % 2], 16)
                for i in range(2):
                    sp.wait_ge(q_stored[i], 16 * NG * T // 2)

            @block.gpsimd
            def _(pool):
                pool.wait_ge(w_hi_done, 1)
                nc.gpsimd.tensor_tensor(w_lo[:], w_raw[:], f32(w_hi[:]), ALU.subtract).then_inc(w_lo_done, 1)

            @block.vector
            def _(dve):
                def split_low(b):
                    dve.wait_ge(xt_hi_done, b + 1)
                    cols = slice(b * NQ, (b + 1) * NQ)
                    nc.vector.tensor_tensor(xt_lo[:, :, cols], xp[b % 2][:, :, 0:NQ], f32(xt_hi[:, :, cols]),
                                            ALU.subtract).then_inc(xt_lo_done, 1)

                chain = Chain(dve, step)
                dve.wait_ge(x_in, 16)
                layernorm_stats(nc, dve, chain, x_all, ln, var_ready, std_ready)
                for b in range(NB):
                    nc.vector.tensor_scalar(x_all[:, b, :], x_all[:, b, :], moments[:, b, 0:1], rstd[:, b:b + 1],
                                            ALU.subtract, ALU.mult).then_inc(xn_ready, 1)
                    if b:
                        split_low(b - 1)
                split_low(NB - 1)
                dve.wait_ge(b_in, 16)
                nc.vector.tensor_scalar(bias_s[:], bias[:], scale, None, ALU.mult).then_inc(bias_done, 1)
                with dve.Fori(0, NG) as g:
                    for t in range(T):
                        n = g * T + t
                        dve.wait_ge(q_val_done, n + 1)
                        dve.wait_ge(q_stored[t % 2], (g * T + t - t % 2) * 8)
                        val = q_val[:, t % 2].rearrange("p (b q) -> p b q", b=CG)
                        nc.vector.tensor_copy(q_out[:, t % 2, :, 0, :], val).then_inc(q_hi_done, 1)
                        dve.wait_ge(q_hi_done, n + 1)
                        nc.vector.tensor_tensor(q_out[:, t % 2, :, 1, :], val, f32(q_out[:, t % 2, :, 0, :]),
                                                ALU.subtract).then_inc(q_lo_done, 1)

            @block.scalar
            def _(act):
                act.wait_ge(w_in, 16)
                nc.scalar.activation(w_hi[:], w_raw[:], ACT.Copy).then_inc(w_hi_done, 1)
                act.wait_ge(var_ready, 1)
                nc.scalar.activation(std[:], veps[:], ACT.Sqrt).then_inc(std_ready, 1)
                for b in range(NB):
                    act.wait_ge(xt_done, b + 1)
                    nc.scalar.activation(xt_hi[:, :, b * NQ:(b + 1) * NQ], xp[b % 2][:, :, 0:NQ],
                                         ACT.Copy).then_inc(xt_hi_done, 1)
                act.wait_ge(bias_done, 1)
                with act.Fori(0, NG) as g:
                    for t in range(T):
                        n = g * T + t
                        act.wait_ge(q_done, n + 1)
                        if t >= 2:
                            act.wait_ge(q_lo_done, n - 1)
                        elif T >= 2:
                            act.wait_ge(q_lo_done, (g * T) * 1 + 0)
                        nc.scalar.activation(q_val[:, t % 2], qp[t % 4][:], ACT.Identity, bias=bias_s[:, t:t + 1],
                                             scale=scale).then_inc(q_val_done, 1)

            @block.tensor
            def _(pe):
                for b in range(NB):
                    pe.wait_ge(xn_ready, b + 1)
                    if b >= 2:
                        pe.wait_ge(xt_lo_done, b - 1)
                    for c in range(DC):
                        last = nc.tensor.transpose(xp[b % 2][:, c, 0:NQ], x_all[:, b, c * P:(c + 1) * P],
                                                   ident[0:NQ, 0:NQ])
                    last.then_inc(xt_done, 1)
                pe.wait_ge(xt_lo_done, NB)
                pe.wait_ge(w_lo_done, 1)
                with pe.Fori(0, NG) as g:
                    cols = bass.ds(g * (CG * NQ), CG * NQ)
                    for t in range(T):
                        if t >= 4:
                            pe.wait_ge(q_val_done, g * T + t - 3)
                        else:
                            pe.wait_ge(q_val_done, g * T)
                        product(nc, qp[t % 4][:], [
                            ((w_hi[:, c, t * P:(t + 1) * P], w_lo[:, c, t * P:(t + 1) * P]),
                             (xt_hi[:, c, cols], xt_lo[:, c, cols])) for c in range(DC)]).then_inc(q_done, 1)


def attention_pass(nc, tag, ident, first_tile, HP, ctx_t, wk_t, wv_t, bk_cols, bv_cols, queries, attended):
    HD = P // HP
    NH = TT * HP
    K = lambda t, h, rel: ("k", t, h, rel)
    V = lambda j: ("v", j, 0, 1)
    TURN = "turn"
    if NH == 8:
        plan = [[K(3, 0, 0), K(3, 1, 0)], [V(0)], [K(0, 0, 1), K(0, 1, 1)], [V(1), V(2)],
                [K(1, 0, 1), K(1, 1, 1)], [V(3)], [K(2, 0, 1), K(2, 1, 1)], [V(4), TURN, V(5)]]
    else:
        plan = [[K(3, 0, 0)], [K(3, 1, 0)], [V(0)], [("a", V(1))],
                [K(0, 0, 1)], [K(0, 1, 1)], [("b", V(1)), ("a", V(2))], [("b", V(2))],
                [K(1, 0, 1)], [K(1, 1, 1)], [V(3)], [("a", V(4))],
                [K(2, 0, 1)], [K(2, 1, 1)], [("b", V(4))], [("a", V(5)), TURN, ("b", V(5))]]
    order = [u[1] if u[0] == "b" else u for slot in plan for u in slot if u != TURN and u[0] != "a"]
    UN = len(order)
    BANKS = 3
    bank_of = {u: n % BANKS for n, u in enumerate(order)}

    def slot_count(b, u):
        return (b + 1) * UN + (order.index(u) - 1)

    def unit_count(b, u):
        return slot_count(b - u[3], u)

    def bank_free(b, u):
        n = order.index(u)
        before = [m for m in range(n) if m % BANKS == n % BANKS]
        if before:
            return slot_count(b, order[before[-1]])
        last = [m for m in range(UN) if m % BANKS == n % BANKS][-1]
        return slot_count(b, order[last]) - UN

    with ExitStack() as ctx:
        st = Stage(nc, ctx, tag)
        wk_hi, wk_lo, wv_hi, wv_lo = (st.sb(n, [P, DC, TW], F32R) for n in ("wk_hi", "wk_lo", "wv_hi", "wv_lo"))
        c_raw = st.sb("c_raw", [P, DC, NKP], F32)
        c_hi = st.sb("c_hi", [P, 2, DC, NKP], F32R)
        c_lo = st.sb("c_lo", [P, 2, DC, NKP], F32R)
        kx = st.sb("kx", [P, 2 * TT, KPAD], F32R)
        k_low = st.sb("k_low", [P, 2, KA], F32R)
        v_hi = st.sb("v_hi", [KR, 2, KT, TW], F32R)
        v_lo = st.sb("v_lo", [KR, 2, KT, TW], F32R)
        q_in = st.sb("q_in", [P, NH, 2, NQ], F32R)
        work = st.sb("work", [P, 4 * TW], F32)
        w_raw = work[:, :].rearrange("p (c n) -> p c n", c=DC)
        probs = work[0:NQ, 0:2 * NKP].rearrange("p (a n) -> p a n", a=2)
        pt_hi = st.sb("pt_hi", [KR, KT, HP, NQ], F32R)
        pt_lo = st.sb("pt_lo", [KR, KT, HP, NQ], F32R)
        o_t = st.sb("o_t", [P, 2, TT, NQ], F32)
        bk = st.sb("bk", [P, TT], F32)
        bv = st.sb("bv", [P, TT], F32)
        neg_max = st.sb("neg_max", [NQ, 2], F32)
        row_sum = st.sb("row_sum", [NQ, 2], F32)
        row_inv = st.sb("row_inv", [NQ, 2], F32)

        sc = st.ps("sc", [P, 2, 512])
        up_all = st.ps("up", [P, BANKS, 512])
        up = [up_all[:, i] for i in range(BANKS)]
        tp = st.ps("tp", [P, 2, 512])
        pv = st.ps("pv", [P, 512])

        w_in, w_hi_done, w_lo_done = st.sem("w_in"), st.sem("w_hi_done"), st.sem("w_lo_done")
        b_in, zeroed = st.sem("b_in"), st.sem("zeroed")
        ctx_in, ctx_hi_done, ctx_split = st.sem("ctx_in"), st.sem("ctx_hi_done"), st.sem("ctx_split")
        unit_done, unit_hi, unit_lo = st.sem("unit_done"), st.sem("unit_hi"), st.sem("unit_lo")
        q_loaded = [st.sem(f"q_loaded{t}") for t in range(TT)]
        k_moved = [st.sem(f"k_moved{t}") for t in range(TT)]
        s_done, max_done, exp_done, inv_done, p_done = (st.sem(n) for n in ("s_done", "max_done", "exp_done", "inv_done", "p_done"))
        t_done, t_hi, t_lo = st.sem("t_done"), st.sem("t_hi"), st.sem("t_lo")
        pv_done, o_done = st.sem("pv_done"), st.sem("o_done")
        o_stored = [st.sem(f"o_stored{i}") for i in range(2)]
        passed = st.sem("passed")

        def head(b, k):
            return b * NH + k

        def group(b, t):
            return b * TT + t

        def slots(b, par, last):
            for k in range(NH):
                tail = par == 1 and k == NH - 1
                yield ("scores", k)
                if k > 0:
                    yield ("turn", b, k - 1)
                elif par == 1:
                    yield ("turn", b - 1, NH - 1)
                for u in plan[k]:
                    if u == TURN:
                        if tail:
                            yield ("turn", b, NH - 1)
                    elif u[0] in "ab":
                        if not (last and u[1][3]):
                            yield ("unit", u[1], u[0])
                    elif not (last and u[3]):
                        yield ("unit", u, "ab")
                if k % HP == 0 and (k > 0 or par == 1):
                    yield ("values", b if k else b - 1, (k // HP - 1) % TT)
                if tail:
                    yield ("values", b, TT - 1)

        def rows_of(j):
            return slice(j * HD, (j + 1) * HD)

        def moved(n):
            return n * (32 * HP)

        first_odd = next(k for k in range(1, NH, 2) if any(K(3, 1, 0) in slot for slot in plan[:k]))

        def scores_at(k, last):
            return up_all[:, 0:2] if last and k % 2 and k >= first_odd else sc

        def reorder(steps):
            out = []
            for s in steps:
                if s[0] == "turn" and out and out[-1][0] == "scores" and s[2] != out[-1][1]:
                    out.insert(len(out) - 1, s)
                else:
                    out.append(s)
            return out

        def batches(eng, program):
            with eng.Fori(0, NB // 2 - 1) as i:
                program(i * 2, 0, False)
                program(i * 2 + 1, 1, False)
            program(NB - 2, 0, False)
            program(NB - 1, 1, True)

        with nc.Block() as block:
            @block.sync
            def _(sp):
                def load_ctx(b):
                    sp.dma_start(c_raw[:], ctx_t[bass.ds(b, 1)].rearrange("o (c p) k -> p (o c) k", p=P)).then_inc(ctx_in, 16)

                def load_q(b, t):
                    for j in range(HP):
                        for r in (j, j ^ 1):
                            sp.dma_start(f32(q_in[rows_of(r), t * HP + j]),
                                         queries[rows_of(j), bass.ds(b, 1), first_tile + t].rearrange("p o a q -> p (o a) q")
                                         ).then_inc(q_loaded[t], 16)

                def move_low(count, u):
                    _, t, half, _ = u
                    lo, n = (0, KA) if half == 0 else (KA, NK - KA)
                    sp.wait_ge(unit_lo, count)
                    for j in range(HP):
                        sp.dma_start(f32(kx[rows_of(j ^ 1), 2 * t + j % 2, lo:lo + n]),
                                     f32(k_low[rows_of(j), half, 0:n])).then_inc(k_moved[t], 16)

                sp.dma_start(w_raw, wk_t.rearrange("(c p) n -> p c n", p=P)).then_inc(w_in, 16)
                load_ctx(0)
                sp.dma_start(bk[:], bk_cols).then_inc(b_in, 16)
                sp.dma_start(bv[:], bv_cols).then_inc(b_in, 16)
                sp.wait_ge(zeroed, 1)
                for t in range(TT):
                    load_q(0, t)
                sp.wait_ge(w_hi_done, 1)
                sp.wait_ge(w_lo_done, 1)
                sp.dma_start(w_raw, wv_t.rearrange("(c p) n -> p c n", p=P)).then_inc(w_in, 16)
                sp.wait_ge(ctx_split, 1)
                load_ctx(1)
                for u in order:
                    if u[3] and u[0] == "k":
                        move_low(slot_count(-1, u), u)

                def program(b, par, last):
                    if not isinstance(b, int):
                        sp.wait_ge(ctx_split, b + 2)
                        load_ctx(b + 2)
                    for s in slots(b, par, last):
                        if s[0] == "scores" and s[1] % HP == HP - 1 and not last:
                            sp.wait_ge(s_done, head(b, s[1]) + 1)
                            load_q(b + 1, s[1] // HP)
                        elif s[0] == "unit" and s[1][0] == "k":
                            move_low(slot_count(b, s[1]), s[1])
                        elif s[0] == "values" and s[2] == TT - 1:
                            vb, vp = s[1], par if s[1] is b else 1 - par
                            sp.wait_ge(o_done, group(vb, TT - 1) + 1)
                            sp.dma_start(attended[:, bass.ds(vb, 1), first_tile:first_tile + TT].rearrange("p o t q -> p (o t) q"),
                                         o_t[:, vp]).then_inc(o_stored[vp], 16)

                batches(sp, program)
                for par in range(2):
                    sp.wait_ge(o_stored[par], 16 * NB // 2)

            @block.gpsimd
            def _(pool):
                def split_ctx(b, par):
                    wait_first(pool, ctx_in, b * 16 + 16, passed)
                    nc.gpsimd.tensor_copy(c_hi[:, par], c_raw[:]).then_inc(ctx_hi_done, 1)
                    pool.wait_ge(ctx_hi_done, b + 1)
                    nc.gpsimd.tensor_tensor(c_lo[:, par], c_raw[:], f32(c_hi[:, par]), ALU.subtract).then_inc(ctx_split, 1)

                split_ctx(1, 1)
                with pool.Fori(1, NB // 2) as i:
                    for par in range(2):
                        b = i * 2 + par
                        pool.wait_ge(unit_done, slot_count(b - 2, K(3, 1, 0)))
                        split_ctx(b, par)

            @block.tensor
            def _(pe):
                def unit(b, u, wait_bank=None, part="ab"):
                    kind, t, half, rel = u
                    par = (par_of[0] + rel) % 2
                    chunks = {"ab": range(DC), "a": range(DC // 2), "b": range(DC // 2, DC)}[part]
                    if wait_bank is not None:
                        pe.wait_ge(unit_lo, wait_bank)
                    out = up[bank_of[u]]
                    if kind == "k":
                        lo, n = (0, KA) if half == 0 else (KA, NK - KA)
                        w = slice(t * P, (t + 1) * P)
                        last = product(nc, out[:, 0:n], [
                            ((wk_hi[:, c, w], wk_lo[:, c, w]), (c_hi[:, par, c, lo:lo + n], c_lo[:, par, c, lo:lo + n]))
                            for c in chunks])
                    else:
                        r = slice(t * KR, (t + 1) * KR)
                        last = product(nc, out[0:KR, :], [
                            ((c_hi[:, par, c, r], c_lo[:, par, c, r]), (wv_hi[:, c, :], wv_lo[:, c, :]))
                            for c in chunks], first="a" in part, final="b" in part)
                    if "b" in part:
                        last.then_inc(unit_done, 1)

                par_of = [1]
                pe.wait_ge(w_hi_done, 1)
                pe.wait_ge(w_lo_done, 1)
                pe.wait_ge(ctx_split, 1)
                seen_v = False
                for n, u in enumerate(sorted((u for u in order if u[3]), key=order.index)):
                    if u[0] == "v" and not seen_v:
                        seen_v = True
                        pe.wait_ge(w_hi_done, 2)
                        pe.wait_ge(w_lo_done, 2)
                    free = bank_free(-1, u)
                    unit(-1, u, free if free > 0 else None)

                def program(b, par, last):
                    par_of[0] = par
                    for s in slots(b, par, last):
                        if s[0] == "scores":
                            k = s[1]
                            t = k // HP
                            g = head(b, k)
                            if k % HP == 0:
                                pe.wait_ge(q_loaded[t], (b + 1) * 32 * HP)
                                pe.wait_ge(k_moved[t], moved(b + 1))
                            if last and k == first_odd:
                                pe.wait_ge(unit_lo, slot_count(b, K(3, 1, 0)))
                            else:
                                pe.wait_ge(exp_done, g - 1 if last and k > first_odd else g)
                            for half in range(2):
                                keys = slice(half * KH, half * KH + KA)
                                for part in (1, 0):
                                    last_mm = nc.tensor.matmul(scores_at(k, last)[0:NQ, half, 0:KA], q_in[:, k, part],
                                                               kx[:, 2 * t + k % 2, keys], start=(part == 1), stop=(part == 0))
                            last_mm.then_inc(s_done, 1)
                        elif s[0] == "turn":
                            g = head(s[1], s[2])
                            pe.wait_ge(p_done, g + 1)
                            pe.wait_ge(t_lo, g)
                            for j in range(KT):
                                mm = nc.tensor.transpose(tp[0:KR, j // 3, (j % 3) * NQ:(j % 3 + 1) * NQ],
                                                         probs[:, s[2] % 2, j * KR:(j + 1) * KR], ident[0:NQ, 0:NQ])
                            mm.then_inc(t_done, 1)
                        elif s[0] == "unit":
                            u, part = s[1:]
                            if u[0] == "v" and u[1] == 0 or u == K(0, 0, 1):
                                pe.wait_ge(ctx_split, b + 2)
                            unit(b, u, bank_free(b, u) if "a" in part else None, part)
                        else:
                            _, vb, t = s
                            vp = par if vb is b else 1 - par
                            cols = slice(t * P, (t + 1) * P)
                            pe.wait_ge(t_lo, head(vb, (t + 1) * HP - 1) + 1)
                            if t == 0:
                                pe.wait_ge(unit_lo, unit_count(vb, V(5)))
                            pe.wait_ge(o_done, group(vb, t))
                            product(nc, pv[:, 0:HP * NQ], [
                                ((v_hi[:, vp, j, cols], v_lo[:, vp, j, cols]), (pt_hi[:, j], pt_lo[:, j]))
                                for j in range(KT)]).then_inc(pv_done, 1)

                batches(pe, program)

            @block.scalar
            def _(act):
                act.wait_ge(w_in, 16)
                nc.scalar.activation(wk_hi[:], w_raw, ACT.Copy).then_inc(w_hi_done, 1)
                act.wait_ge(ctx_in, 16)
                nc.scalar.activation(c_hi[:, 0], c_raw[:], ACT.Copy).then_inc(ctx_hi_done, 1)
                act.wait_ge(w_in, 32)
                nc.scalar.activation(wv_hi[:], w_raw, ACT.Copy).then_inc(w_hi_done, 1)
                act.wait_ge(b_in, 32)

                def unit(count, u, par):
                    kind, t, half, rel = u
                    act.wait_ge(unit_done, count)
                    if kind == "k":
                        lo, n = (0, KA) if half == 0 else (KA, NK - KA)
                        for odd in range(2):
                            ins = nc.scalar.activation(kx[:, 2 * t + odd, lo:lo + n], up[bank_of[u]][:, 0:n],
                                                       ACT.Identity, bias=bk[:, t:t + 1])
                    else:
                        ins = nc.scalar.activation(v_hi[:, (par + rel) % 2, t], up[bank_of[u]][0:KR, :], ACT.Copy)
                    ins.then_inc(unit_hi, 1)

                for u in order:
                    if u[3]:
                        unit(slot_count(-1, u), u, 1)

                def program(b, par, last):
                    steps = list(slots(b, par, last))
                    for s in reorder(steps):
                        if s[0] == "scores":
                            k = s[1]
                            g = head(b, k)
                            act.wait_ge(max_done, g + 1)
                            nc.scalar.activation(probs[:, k % 2, 0:NK].rearrange("p (a n) -> p a n", a=2),
                                                 scores_at(k, last)[0:NQ, :, 0:KH], ACT.Exp, bias=neg_max[:, k % 2:k % 2 + 1],
                                                 accum_out=row_sum[:, k % 2:k % 2 + 1]).then_inc(exp_done, 1)
                        elif s[0] == "turn":
                            g = head(s[1], s[2])
                            act.wait_ge(t_done, g + 1)
                            nc.scalar.activation(pt_hi[:, :, s[2] % HP, :].rearrange("p (a j) q -> p a j q", a=2),
                                                 tp[0:KR, :, 0:3 * NQ].rearrange("p a (j q) -> p a j q", j=3),
                                                 ACT.Copy).then_inc(t_hi, 1)
                        elif s[0] == "unit" and "b" in s[2]:
                            unit(slot_count(b, s[1]), s[1], par)

                batches(act, program)

            @block.vector
            def _(dve):
                nc.vector.memset(f32(q_in[:]), 0.0)
                nc.vector.memset(f32(kx[:, :, NK:KPAD]), 0.0).then_inc(zeroed, 1)
                dve.wait_ge(w_hi_done, 1)
                nc.vector.tensor_tensor(wk_lo[:], w_raw, f32(wk_hi[:]), ALU.subtract).then_inc(w_lo_done, 1)
                dve.wait_ge(ctx_hi_done, 1)
                nc.vector.tensor_tensor(c_lo[:, 0], c_raw[:], f32(c_hi[:, 0]), ALU.subtract).then_inc(ctx_split, 1)
                dve.wait_ge(w_hi_done, 2)
                nc.vector.tensor_tensor(wv_lo[:], w_raw, f32(wv_hi[:]), ALU.subtract).then_inc(w_lo_done, 1)
                dve.wait_ge(w_lo_done, 2)
                nc.vector.memset(probs[:, :, NK:NKP], 0.0).then_inc(zeroed, 1)
                dve.wait_ge(b_in, 32)

                def unit(b, u, par):
                    kind, t, half, rel = u
                    dve.wait_ge(unit_hi, slot_count(b, u))
                    if kind == "k":
                        lo, n = (0, KA) if half == 0 else (KA, NK - KA)
                        before = b + rel if t == 0 else b + rel + 1
                        if not isinstance(before, int) or before > 0:
                            dve.wait_ge(k_moved[(t - 1) % TT], moved(before))
                        ins = nc.vector.scalar_tensor_tensor(out=k_low[:, half, 0:n], in0=up[bank_of[u]][:, 0:n],
                                                             scalar=bk[:, t:t + 1], in1=f32(kx[:, 2 * t, lo:lo + n]),
                                                             op0=ALU.add, op1=ALU.subtract)
                    else:
                        vp = (par + rel) % 2
                        ins = nc.vector.tensor_tensor(v_lo[:, vp, t], up[bank_of[u]][0:KR, :], f32(v_hi[:, vp, t]),
                                                      ALU.subtract)
                    ins.then_inc(unit_lo, 1)

                for u in order:
                    if u[3]:
                        unit(-1, u, 1)

                def normalise(b, k):
                    g = head(b, k)
                    dve.wait_ge(exp_done, g + 1)
                    nc.vector.reciprocal(row_inv[:, k % 2:k % 2 + 1], row_sum[:, k % 2:k % 2 + 1]).then_inc(inv_done, 1)
                    dve.wait_ge(inv_done, g + 1)
                    nc.vector.tensor_scalar(probs[:, k % 2, 0:NK], probs[:, k % 2, 0:NK], row_inv[:, k % 2:k % 2 + 1],
                                            None, ALU.mult).then_inc(p_done, 1)

                def program(b, par, last):
                    waiting = None
                    for s in slots(b, par, last):
                        if s[0] == "scores":
                            k = s[1]
                            g = head(b, k)
                            dve.wait_ge(s_done, g + 1)
                            nc.vector.tensor_reduce(neg_max[:, k % 2:k % 2 + 1], scores_at(k, last)[0:NQ, :, 0:KH],
                                                    mybir.AxisListType.XY, ALU.max, negate=True).then_inc(max_done, 1)
                            waiting = k
                            if k == 0 and par == 0:
                                normalise(b, k)
                                waiting = None
                        elif s[0] == "turn":
                            g = head(s[1], s[2])
                            dve.wait_ge(t_hi, g + 1)
                            h = s[2] % HP
                            nc.vector.tensor_tensor(pt_lo[:, :, h, :].rearrange("p (a j) q -> p a j q", a=2),
                                                    tp[0:KR, :, 0:3 * NQ].rearrange("p a (j q) -> p a j q", j=3),
                                                    f32(pt_hi[:, :, h, :]).rearrange("p (a j) q -> p a j q", a=2),
                                                    ALU.subtract).then_inc(t_lo, 1)
                            if waiting is not None:
                                normalise(b, waiting)
                                waiting = None
                        elif s[0] == "unit" and "b" in s[2]:
                            unit(b, s[1], par)
                        elif s[0] == "values":
                            _, vb, t = s
                            op = par if vb is b else 1 - par
                            dve.wait_ge(pv_done, group(vb, t) + 1)
                            if t == 0:
                                dve.wait_ge(o_stored[op], pair_of(vb, op) * 16)
                            for j in range(HP):
                                rows = slice(j * HD, (j + 1) * HD)
                                ins = nc.vector.tensor_scalar(o_t[rows, op, t, :], pv[rows, j * NQ:(j + 1) * NQ],
                                                              bv[rows, t:t + 1], None, ALU.add)
                            ins.then_inc(o_done, 1)

                def pair_of(b, par):
                    return pair[0]

                pair = [0]
                with dve.Fori(0, NB // 2 - 1) as i:
                    pair[0] = i
                    program(i * 2, 0, False)
                    program(i * 2 + 1, 1, False)
                pair[0] = NB // 2 - 1
                program(NB - 2, 0, False)
                program(NB - 1, 1, True)


def output_stage(nc, tag, ident, x_rows, wo_t, bo, attended, wg, bg_cols, acc, table, logits_t, logits, gated):
    T = wo_t.shape[0] // P
    CG = 4
    NG = NB // CG
    with ExitStack() as ctx:
        st = Stage(nc, ctx, tag)
        x_all = st.sb("x", [NQ, NB, D], F32)
        ln = layernorm_buffers(st)
        stats, moments, veps, std, rstd, _ = ln
        bo_all = st.sb("bo", [NQ, D], F32)
        zero = st.sb("zero", [NQ, TABLE_W], F32)
        g_raw = st.sb("g_raw", [P, DC, P], F32)
        g_hi = st.sb("g_hi", [P, DC, P], F32R)
        g_lo = st.sb("g_lo", [P, DC, P], F32R)
        bg = st.sb("bg", [P, 1], F32)
        step = st.sem("step")
        x_in, w_in, b_in, o_in = st.sem("x_in"), st.sem("w_in"), st.sem("b_in"), [st.sem(f"o_in{i}") for i in range(2)]
        passed = st.sem("passed")
        with ExitStack() as inner:
            it = Stage(nc, inner, tag + "a")
            w_raw = it.sb("w_raw", [P, T, D], F32)
            w_hi = it.sb("w_hi", [P, T, D], F32R)
            w_lo = it.sb("w_lo", [P, T, D], F32R)
            o_raw = it.sb("o_raw", [P, 2, T, NQ], F32)
            o_hi = it.sb("o_hi", [P, 2, T, NQ], F32R)
            o_lo = it.sb("o_lo", [P, 2, T, NQ], F32R)
            yp = [it.ps(f"yp{i}", [P, D]) for i in range(2)]
            w_hi_done, w_lo_done, g_hi_done, g_lo_done = (it.sem(n) for n in ("w_hi_done", "w_lo_done", "g_hi_done", "g_lo_done"))
            o_hi_done, o_lo_done, x_biased = (it.sem(n) for n in ("o_hi_done", "o_lo_done", "x_biased"))
            y_done, y_read = ([it.sem(f"{n}{i}") for i in range(2)] for n in ("y_done", "y_read"))
            with nc.Block() as block:
                @block.sync
                def _(sp):
                    sp.dma_start(w_raw[:], wo_t.rearrange("(t p) n -> p t n", p=P)).then_inc(w_in, 16)
                    sp.dma_start(bo_all[:], bo.partition_broadcast(NQ)).then_inc(b_in, 16)
                    sp.dma_start(g_raw[:], wg.rearrange("(c p) n -> p c n", p=P)).then_inc(b_in, 16)
                    sp.dma_start(bg[:], bg_cols).then_inc(b_in, 16)
                    sp.dma_start(x_all[:], x_rows.rearrange("(b p) d -> p b d", p=NQ)).then_inc(x_in, 16)
                    with sp.Fori(0, NB // 2) as i:
                        for par in range(2):
                            b = i * 2 + par
                            sp.wait_ge(o_lo_done, i * 2)
                            sp.dma_start(o_raw[:, par], attended[:, bass.ds(b, 1)].rearrange("p o t q -> p (o t) q")
                                         ).then_inc(o_in[par], 16)

                @block.gpsimd
                def _(pool):
                    wait_first(pool, x_in, 16, passed)
                    wait_first(pool, b_in, 48, passed)
                    nc.gpsimd.tensor_tensor(x_all[:], x_all[:], bo_all[:, :].unsqueeze(1).broadcast_to([NQ, NB, D]),
                                            ALU.add).then_inc(x_biased, 1)
                    nc.gpsimd.tensor_copy(g_hi[:], g_raw[:]).then_inc(g_hi_done, 1)
                    pool.wait_ge(g_hi_done, 1)
                    nc.gpsimd.tensor_tensor(g_lo[:], g_raw[:], f32(g_hi[:]), ALU.subtract).then_inc(g_lo_done, 1)
                    pool.wait_ge(g_lo_done, 1)

                @block.scalar
                def _(act):
                    act.wait_ge(w_in, 16)
                    nc.scalar.activation(w_hi[:], w_raw[:], ACT.Copy).then_inc(w_hi_done, 1)
                    with act.Fori(0, NB // 2) as i:
                        for par in range(2):
                            act.wait_ge(o_in[par], i * 16 + 16)
                            act.wait_ge(y_done[par], i)
                            nc.scalar.activation(o_hi[:, par], o_raw[:, par], ACT.Copy).then_inc(o_hi_done, 1)

                @block.vector
                def _(dve):
                    nc.vector.memset(zero[:], 0.0)
                    dve.wait_ge(w_hi_done, 1)
                    nc.vector.tensor_tensor(w_lo[:], w_raw[:], f32(w_hi[:]), ALU.subtract).then_inc(w_lo_done, 1)

                    def split(b, par):
                        dve.wait_ge(o_hi_done, b + 1)
                        nc.vector.tensor_tensor(o_lo[:, par], o_raw[:, par], f32(o_hi[:, par]),
                                                ALU.subtract).then_inc(o_lo_done, 1)

                    def add(i, par):
                        dve.wait_ge(y_done[par], i + 1)
                        cur = x_all[:, bass.ds(i * 2 + par, 1)].rearrange("p o d -> p (o d)")
                        nc.vector.tensor_tensor(cur, yp[par][0:NQ, :], cur, ALU.add).then_inc(y_read[par], 1)

                    split(0, 0)
                    dve.wait_ge(x_biased, 1)
                    with dve.Fori(0, NB // 2 - 1) as i:
                        split(i * 2 + 1, 1)
                        add(i, 0)
                        split(i * 2 + 2, 0)
                        add(i, 1)
                    split(NB - 1, 1)
                    add(NB // 2 - 1, 0)
                    add(NB // 2 - 1, 1)

                @block.tensor
                def _(pe):
                    pe.wait_ge(w_hi_done, 1)
                    pe.wait_ge(w_lo_done, 1)
                    with pe.Fori(0, NB // 2) as i:
                        for par in range(2):
                            b = i * 2 + par
                            pe.wait_ge(o_lo_done, b + 1)
                            pe.wait_ge(y_read[par], i)
                            product(nc, yp[par][0:NQ, :], [
                                ((o_hi[:, par, t], o_lo[:, par, t]), (w_hi[:, t], w_lo[:, t])) for t in range(T)
                            ]).then_inc(y_done[par], 1)

        with ExitStack() as inner:
            it = Stage(nc, inner, tag + "b")
            xn = it.sb("xn", [NQ, NB, D], F32)
            xt_hi = it.sb("xt_hi", [P, DC, NT], F32R)
            xt_lo = it.sb("xt_lo", [P, DC, NT], F32R)
            xp = [it.ps(f"xp{i}", [P, DC, P]) for i in range(2)]
            lp = [it.ps(f"lp{i}", [P, CG * NQ]) for i in range(2)]
            tp = it.ps("tp", [P, NB, E])
            soft = it.sb("soft", [NQ, NB, E], F32)
            top = it.sb("top", [NQ, NB], F32)
            total = it.sb("total", [NQ, NB], F32)
            gate = it.sb("gate", [NQ, NB], F32)
            gates = it.sb("gates", [NQ, NB, E], F32)
            stored = it.sem("stored")
            var_ready, std_ready = it.sem("var_ready"), it.sem("std_ready")
            xn_ready, xt_done, xt_hi_done, xt_lo_done = (it.sem(n) for n in ("xn_ready", "xt_done", "xt_hi_done", "xt_lo_done"))
            l_done, l_copied, lt_done, lt_copied = (it.sem(n) for n in ("l_done", "l_copied", "lt_done", "lt_copied"))
            shifted, gates_ready, rows_ready = it.sem("shifted"), it.sem("gates_ready"), it.sem("rows_ready")
            soft_ready = it.sem("soft_ready")
            with nc.Block() as block:
                @block.sync
                def _(sp):
                    rows = lambda t, w: t[0:NT, w].rearrange("(b p) d -> p b d", p=NQ)
                    sp.dma_start(rows(acc, slice(0, D)), x_all[:]).then_inc(stored, 16)
                    for r in range(SLOT_MAX // NQ):
                        at = slice(NT + r * NQ, NT + (r + 1) * NQ)
                        sp.dma_start(acc[at, :], zero[:, 0:D]).then_inc(stored, 16)
                        sp.dma_start(table[at, :], zero[:]).then_inc(stored, 16)
                    sp.wait_ge(rows_ready, 1)
                    sp.dma_start(rows(table, slice(0, D)), xn[:]).then_inc(stored, 16)
                    sp.wait_ge(gates_ready, 1)
                    with nc.allow_non_contiguous_dma(reason="eight gates at the end of each row"):
                        sp.dma_start(rows(table, slice(D, TABLE_W)), gates[:]).then_inc(stored, 16)
                    sp.wait_ge(stored, 16 * (3 + 2 * (SLOT_MAX // NQ)))

                @block.vector
                def _(dve):
                    chain = Chain(dve, step)
                    layernorm_stats(nc, dve, chain, x_all, ln, var_ready, std_ready)

                    def split_low(b):
                        dve.wait_ge(xt_hi_done, b + 1)
                        cols = slice(b * NQ, (b + 1) * NQ)
                        nc.vector.tensor_tensor(xt_lo[:, :, cols], xp[b % 2][:, :, 0:NQ], f32(xt_hi[:, :, cols]),
                                                ALU.subtract).then_inc(xt_lo_done, 1)

                    for b in range(NB):
                        nc.vector.tensor_scalar(xn[:, b, :], x_all[:, b, :], moments[:, b, 0:1], rstd[:, b:b + 1],
                                                ALU.subtract, ALU.mult).then_inc(xn_ready, 1)
                        if b:
                            split_low(b - 1)
                    split_low(NB - 1)
                    if not gated:
                        dve.wait_ge(xn_ready, NB)
                        chain.step(nc.vector.tensor_copy(top[:, 0:1], xn[:, 0, 0:1]))
                        nc.vector.memset(total[:], 0.0).then_inc(rows_ready, 1)
                    for g in range(NG):
                        dve.wait_ge(l_done, g + 1)
                        nc.vector.tensor_scalar(logits_t[:, g * CG * NQ:(g + 1) * CG * NQ], lp[g % 2][:], bg[:, 0:1], None,
                                                ALU.add).then_inc(l_copied, 1)
                    dve.wait_ge(lt_done, 1)
                    nc.vector.tensor_copy(logits[:], tp[0:NQ]).then_inc(lt_copied, 1)
                    if gated:
                        dve.wait_ge(lt_copied, 1)
                        chain.link(nc.vector.tensor_reduce(top[:], logits[:], AX_X, ALU.max))
                        nc.vector.tensor_tensor(soft[:], logits[:], top[:, :].unsqueeze(2).broadcast_to([NQ, NB, E]),
                                                ALU.subtract).then_inc(shifted, 1)
                        dve.wait_ge(soft_ready, 1)
                        chain.link(nc.vector.tensor_reduce(total[:], soft[:], AX_X, ALU.add))
                        chain.link(nc.vector.reciprocal(gate[:], total[:]))
                        nc.vector.tensor_copy(gates[:], gate[:, :].unsqueeze(2).broadcast_to([NQ, NB, E])).then_inc(gates_ready, 1)
                        for b in range(NB):
                            ins = nc.vector.tensor_scalar(xn[:, b, :], xn[:, b, :], gate[:, b:b + 1], None, ALU.mult)
                        ins.then_inc(rows_ready, 1)

                @block.scalar
                def _(act):
                    act.wait_ge(var_ready, 1)
                    nc.scalar.activation(std[:], veps[:], ACT.Sqrt).then_inc(std_ready, 1)
                    for b in range(NB):
                        act.wait_ge(xt_done, b + 1)
                        nc.scalar.activation(xt_hi[:, :, b * NQ:(b + 1) * NQ], xp[b % 2][:, :, 0:NQ],
                                             ACT.Copy).then_inc(xt_hi_done, 1)
                    if gated:
                        act.wait_ge(shifted, 1)
                        nc.scalar.activation(soft[:], soft[:], ACT.Exp).then_inc(soft_ready, 1)
                    else:
                        act.wait_ge(lt_copied, 1)
                        nc.scalar.activation(gates[:], logits[:], ACT.Sigmoid).then_inc(gates_ready, 1)

                @block.tensor
                def _(pe):
                    for b in range(NB):
                        pe.wait_ge(xn_ready, b + 1)
                        if b >= 2:
                            pe.wait_ge(xt_lo_done, b - 1)
                        for c in range(DC):
                            last = nc.tensor.transpose(xp[b % 2][:, c, 0:NQ], xn[:, b, c * P:(c + 1) * P],
                                                       ident[0:NQ, 0:NQ])
                        last.then_inc(xt_done, 1)
                    for g in range(NG):
                        pe.wait_ge(xt_lo_done, CG * (g + 1))
                        if g >= 2:
                            pe.wait_ge(l_copied, g - 1)
                        cols = slice(g * CG * NQ, (g + 1) * CG * NQ)
                        product(nc, lp[g % 2][:], [((g_hi[:, c], g_lo[:, c]), (xt_hi[:, c, cols], xt_lo[:, c, cols]))
                                                   for c in range(DC)]).then_inc(l_done, 1)
                    pe.wait_ge(l_copied, NG)
                    for b in range(NB):
                        last = nc.tensor.transpose(tp[0:NQ, b], logits_t[0:E, b * NQ:(b + 1) * NQ], ident[0:E, 0:E])
                    last.then_inc(lt_done, 1)


def route_stage(nc, tag, ident, logits_t, logits, choose, slots, capacity, slot_rows):
    NS = slots // NQ
    EXP_ONES = 0x7F800000
    with ExitStack() as ctx:
        st = Stage(nc, ctx, tag)
        tri = st.sb("tri", [NQ, NQ], BF16)
        ones = st.sb("ones", [NQ, NQ], BF16)
        slot_id = st.sb("slot_id", [NQ, slots], F16)
        token = st.sb("token", [NQ, NB, 2], F16)
        dummy = st.sb("dummy", [NQ, NS], F32)
        chosen = st.sb("chosen", [NQ, NB, E], BF16)
        place = st.sb("place", [NQ, NB, E], F32)
        hot = st.sb("hot", [NQ, 2, NB, slots], F16)
        count_ps = st.ps("count_ps", [P, NB, E])
        rows_ps = st.ps("rows_ps", [P, E * NS, 2])
        tmp = st.sb("tmp", [NQ, NB, E], F32)
        tmp2 = st.sb("tmp2", [NQ, E, NS], F32)
        tmp3 = st.sb("tmp3", [NQ, E, NS], F32)
        step, made, counted, placed = st.sem("step"), st.sem("made"), st.sem("counted"), st.sem("placed")
        chosen_ready = st.sem("chosen_ready")
        hot_ready, hot_used, rows_done = st.sem("hot_ready"), st.sem("hot_used"), st.sem("rows_done")
        consts, zero_made, out_ready = st.sem("consts"), st.sem("zero_made"), st.sem("out_ready")
        if choose == "tokens":
            diff = st.sb("diff", [P, P], I32)
            same = st.sb("same", [P, P], BF16)
            lane = st.sb("lane", [P, 1], I32)
            lane_f = st.sb("lane_f", [P, 1], F32)
            part = st.sb("part", [P, 8], I32)
            prefix = st.sb("prefix", [P, 1], I32)
            cand = st.sb("cand", [P, 3], I32)
            cnt = st.sb("cnt", [P, 1], F32)
            enough = st.sb("enough", [P, 1], BF16)
            digit = st.sb("digit", [P, 2], I32)
            seen = st.sb("seen", [P, NT], BF16)
            cut = st.sb("cut", [P, 2 * E], F32)
            cut_tok = st.sb("cut_tok", [NQ, 2 * E], F32)
            ones_f = st.sb("ones_f", [E, NQ], F32)
            eq = st.sb("eq", [NQ, NB, E], BF16)
            gt = st.sb("gt", [NQ, NB, E], F32)
            sum_ps = st.ps("sum_ps", [P, 8])
            cut_ps = st.ps("cut_ps", [P, 2 * E])
            enough_ready, digit_ready, cut_ready, cut_done = (st.sem(n) for n in ("enough_ready", "digit_ready", "cut_ready", "cut_done"))
            eq_ready = st.sem("eq_ready")
        else:
            rank = st.sb("rank", [NQ, NB, E], F32)
            top = st.sb("top", [NQ, NB], F32)

        counts = 2 if choose == "tokens" else 1

        def running_count(pe, mask, done):
            nc.tensor.matmul(count_ps[0:NQ], tri[:], mask[:], start=True, stop=False)
            for b in range(NB - 1):
                rest = NB - 1 - b
                last = nc.tensor.matmul(count_ps[0:NQ, b + 1:NB, :], ones[:],
                                        mask[:, b:b + 1, :].broadcast_to([NQ, rest, E]),
                                        start=False, stop=(b == NB - 2))
            last.then_inc(done, 1)

        def search(dve, chain):
            chain.link(nc.vector.tensor_scalar(diff[:], diff[:], E - 1, None, ALU.bitwise_and))
            chain.link(nc.vector.tensor_scalar(same[:], diff[:], 0, None, ALU.is_equal))
            chain.link(nc.vector.memset(same[0:E, :], 0.0))
            chain.link(nc.vector.tensor_scalar(lane[:], lane[:], 3, None, ALU.logical_shift_right))
            chain.link(nc.vector.tensor_copy(lane_f[:], lane[:]))
            chain.link(nc.vector.tensor_scalar(lane_f[:], lane_f[:], float(E - 1), None, ALU.min))
            for j in range(8):
                ins = nc.vector.tensor_scalar(part[:, j:j + 1], lane[:], 28 - 4 * j, None, ALU.logical_shift_left)
            chain.step(ins)
            chain.link(nc.vector.memset(prefix[:], 0))

            def as_float():
                chain.link(nc.vector.tensor_scalar(cand[:, 1:2], cand[:, 0:1], 31, -1, ALU.arith_shift_right, ALU.bitwise_xor))
                chain.link(nc.vector.tensor_scalar(cand[:, 1:2], cand[:, 1:2], -2147483648, None, ALU.bitwise_or))
                chain.link(nc.vector.tensor_tensor(cand[:, 2:3], cand[:, 0:1], cand[:, 1:2], ALU.bitwise_xor))

            def finite():
                chain.link(nc.vector.tensor_scalar(cand[:, 0:1], cand[:, 2:3], EXP_ONES, None, ALU.bitwise_and))
                chain.link(nc.vector.tensor_scalar(cand[:, 0:1], cand[:, 0:1], float(EXP_ONES), -1.0, ALU.is_equal, ALU.mult))
                chain.link(nc.vector.tensor_scalar(cand[:, 1:2], cand[:, 0:1], 0x7FFFFF, None, ALU.bitwise_and))
                chain.link(nc.vector.tensor_scalar(cand[:, 0:1], cand[:, 0:1], 0x800000, None, ALU.bitwise_and))
                chain.link(nc.vector.tensor_tensor(cand[:, 2:3], cand[:, 2:3], cand[:, 1:2], ALU.bitwise_or))
                chain.link(nc.vector.tensor_tensor(cand[:, 2:3], cand[:, 2:3], cand[:, 0:1], ALU.bitwise_xor))

            for j in range(8):
                chain.link(nc.vector.tensor_tensor(cand[:, 0:1], prefix[:], part[:, j:j + 1], ALU.bitwise_or))
                as_float()
                if j < 3:
                    finite()
                chain.link(nc.vector.tensor_scalar(seen[:], logits_t[:], f32(cand[:, 2:3]), 0.0, ALU.is_ge, ALU.add,
                                                   accum_out=cnt[:]))
                nc.vector.tensor_scalar(enough[:], cnt[:], float(slots), None, ALU.is_ge).then_inc(enough_ready, 1)
                dve.wait_ge(digit_ready, j + 1)
                chain.link(nc.vector.tensor_copy(digit[:, 0:1], sum_ps[:, j:j + 1]))
                chain.link(nc.vector.tensor_scalar(digit[:, 1:2], digit[:, 0:1], 28 - 4 * j, None, ALU.logical_shift_left))
                chain.link(nc.vector.tensor_tensor(prefix[:], prefix[:], digit[:, 1:2], ALU.bitwise_or))
            chain.link(nc.vector.tensor_tensor(cand[:, 0:1], prefix[:], prefix[:], ALU.bitwise_or))
            as_float()
            finite()
            chain.link(nc.vector.tensor_scalar(seen[:], logits_t[:], f32(cand[:, 2:3]), 0.0, ALU.is_gt, ALU.add,
                                               accum_out=cnt[:]))
            chain.link(nc.vector.tensor_scalar(cnt[:], cnt[:], -1.0, float(slots), ALU.mult, ALU.add))
            chain.link(nc.vector.tensor_scalar(cut[0:E, 0:E], ident[0:E, 0:E], f32(cand[0:E, 2:3]), None, ALU.mult))
            chain.link(nc.vector.tensor_scalar(cut[0:E, E:2 * E], ident[0:E, 0:E], cnt[0:E], None, ALU.mult))
            nc.vector.memset(ones_f[:], 1.0).then_inc(cut_ready, 1)
            dve.wait_ge(cut_done, 1)
            chain.link(nc.vector.tensor_copy(cut_tok[:], cut_ps[0:NQ]))
            value = cut_tok[:, 0:E].unsqueeze(1).broadcast_to([NQ, NB, E])
            quota = cut_tok[:, E:2 * E].unsqueeze(1).broadcast_to([NQ, NB, E])
            nc.vector.tensor_tensor(eq[:], logits[:], value, ALU.is_equal).then_inc(eq_ready, 1)
            chain.link(nc.vector.tensor_tensor(gt[:], logits[:], value, ALU.is_gt))
            dve.wait_ge(counted, 1)
            chain.link(nc.vector.tensor_tensor(tmp[:], count_ps[0:NQ], quota, ALU.is_le))
            chain.link(nc.vector.tensor_tensor(tmp[:], tmp[:], eq[:], ALU.mult))
            nc.vector.tensor_tensor(chosen[:], tmp[:], gt[:], ALU.add).then_inc(chosen_ready, 1)

        with nc.Block() as block:
            @block.gpsimd
            def _(pool):
                nc.gpsimd.memset(tri[:], 1.0).then_inc(zero_made, 1)
                nc.gpsimd.memset(ones[:], 1.0).then_inc(consts, 1)
                pool.wait_ge(zero_made, 1)
                nc.gpsimd.affine_select(out=tri[:], in_=tri[:], compare_op=ALU.is_ge, fill=0.0, base=0,
                                        pattern=[[1, NQ]], channel_multiplier=-1).then_inc(consts, 1)
                nc.gpsimd.iota(slot_id[:], pattern=[[1, slots]], base=1, channel_multiplier=0,
                               allow_small_or_imprecise_dtypes=True).then_inc(consts, 1)
                nc.gpsimd.iota(token[:, :, 0], pattern=[[NQ, NB]], base=0, channel_multiplier=1,
                               allow_small_or_imprecise_dtypes=True).then_inc(consts, 1)
                nc.gpsimd.memset(token[:, :, 1], 1.0).then_inc(consts, 1)
                nc.gpsimd.iota(dummy[:], pattern=[[NQ, NS]], base=NT, channel_multiplier=1,
                               allow_small_or_imprecise_dtypes=True).then_inc(consts, 1)
                if choose == "tokens":
                    nc.gpsimd.iota(diff[:], pattern=[[-1, P]], base=P, channel_multiplier=1).then_inc(consts, 1)
                    nc.gpsimd.iota(lane[:], pattern=[[0, 1]], base=0, channel_multiplier=1).then_inc(consts, 1)
                else:
                    nc.gpsimd.iota(rank[:], pattern=[[0, NB], [-1, E]], base=E, channel_multiplier=0,
                                   allow_small_or_imprecise_dtypes=True).then_inc(consts, 1)
            NCONST = 8 if choose == "tokens" else 7

            @block.vector
            def _(dve):
                chain = Chain(dve, step)
                dve.wait_ge(consts, NCONST)
                if choose == "tokens":
                    search(dve, chain)
                else:
                    chain.link(nc.vector.tensor_reduce(top[:], logits[:], AX_X, ALU.max))
                    chain.link(nc.vector.tensor_tensor(tmp[:], logits[:], top[:, :].unsqueeze(2).broadcast_to([NQ, NB, E]),
                                                       ALU.is_equal))
                    chain.link(nc.vector.tensor_tensor(tmp[:], tmp[:], rank[:], ALU.mult))
                    chain.link(nc.vector.tensor_reduce(top[:], tmp[:], AX_X, ALU.max))
                    nc.vector.tensor_tensor(chosen[:], rank[:], top[:, :].unsqueeze(2).broadcast_to([NQ, NB, E]),
                                            ALU.is_equal).then_inc(chosen_ready, 1)
                dve.wait_ge(chosen_ready, 1)
                dve.wait_ge(counted, counts)
                chain.link(nc.vector.tensor_tensor(place[:], count_ps[0:NQ], chosen[:], ALU.mult))
                if capacity is not None:
                    chain.link(nc.vector.scalar_tensor_tensor(out=place[:], in0=place[:], scalar=float(capacity),
                                                              in1=place[:], op0=ALU.is_lt, op1=ALU.mult))
                for e in range(E):
                    if e >= 2:
                        dve.wait_ge(hot_used, e - 1)
                    for b in range(NB):
                        ins = nc.vector.tensor_scalar(hot[:, e % 2, b], slot_id[:], place[:, b, e:e + 1], None, ALU.is_equal)
                    ins.then_inc(hot_ready, 1)
                dve.wait_ge(hot_used, E)
                ps = rows_ps[0:NQ].rearrange("p (e s) c -> p e s c", e=E)
                dm = dummy[:, :].unsqueeze(1).broadcast_to([NQ, E, NS])
                chain.link(nc.vector.tensor_tensor(tmp2[:], ps[:, :, :, 1], dm, ALU.mult))
                chain.link(nc.vector.tensor_tensor(tmp3[:], dm, tmp2[:], ALU.subtract))
                chain.link(nc.vector.tensor_tensor(tmp2[:], ps[:, :, :, 0], tmp3[:], ALU.add))
                chain.link(nc.vector.tensor_copy(slot_rows[:, 0:E * NS].rearrange("p (e s) -> p e s", e=E), tmp2[:]))
                chain.link(nc.vector.tensor_copy(slot_rows[:, E * NS:(E + 1) * NS], tmp2[:, 0, :]))

            @block.tensor
            def _(pe):
                pe.wait_ge(consts, NCONST)
                if choose == "tokens":
                    for j in range(8):
                        pe.wait_ge(enough_ready, j + 1)
                        nc.tensor.matmul(sum_ps[:, j:j + 1], same[:], enough[:], start=True, stop=True).then_inc(digit_ready, 1)
                    pe.wait_ge(cut_ready, 1)
                    nc.tensor.matmul(cut_ps[0:NQ], ones_f[:], cut[0:E], start=True, stop=True).then_inc(cut_done, 1)
                    pe.wait_ge(eq_ready, 1)
                    running_count(pe, eq, counted)
                pe.wait_ge(chosen_ready, 1)
                running_count(pe, chosen, counted)
                for e in range(E):
                    pe.wait_ge(hot_ready, e + 1)
                    for s in range(NS):
                        for b in range(NB):
                            last = nc.tensor.matmul(rows_ps[0:NQ, e * NS + s, :], hot[:, e % 2, b, s * NQ:(s + 1) * NQ],
                                                    token[:, b, :], start=(b == 0), stop=(b == NB - 1))
                    last.then_inc(hot_used, 1)


def ffn_stage(nc, tag, ident, table, acc, slot_rows, w1, b1_cols, w2, b2, slots, act_func):
    NS = slots // NQ
    FF = w1.shape[2]
    FQ = 4
    NQD = FF // (FQ * P)
    FT = FQ * NQD
    with ExitStack() as ctx:
        st = Stage(nc, ctx, tag)
        w1_raw = st.sb("w1_raw", [P, 2, DC, FQ * P], F32)
        w2_raw = st.sb("w2_raw", [P, 2, FQ, D], F32)
        w1_hi, w1_lo = st.sb("w1_hi", [P, 2, DC, FQ * P], F32R), st.sb("w1_lo", [P, 2, DC, FQ * P], F32R)
        w2_hi, w2_lo = st.sb("w2_hi", [P, 2, FQ, D], F32R), st.sb("w2_lo", [P, 2, FQ, D], F32R)
        b1 = st.sb("b1", [P, E * FT], F32)
        b2_all = st.sb("b2", [NQ, 2, D], F32)
        rows_now = st.sb("rows_now", [NQ, 2, NS], U32)
        xg = st.sb("xg", [NQ, 2, NS, TABLE_W], F32)
        xe_hi = st.sb("xe_hi", [P, 2, DC, slots], F32R)
        xe_lo = st.sb("xe_lo", [P, 2, DC, slots], F32R)
        h_val = st.sb("h_val", [P, 2, slots], F32)
        h_hi = st.sb("h_hi", [P, 2, slots], F32R)
        h_lo = st.sb("h_lo", [P, 2, slots], F32R)
        y_val = st.sb("y_val", [NQ, NS, D], F32)
        yp = [st.ps(f"yp{s}", [P, D]) for s in range(NS)]
        hp = [st.ps(f"hp{i}", [P, slots]) for i in range(2)]
        xp = [st.ps(f"xp{i}", [P, DC, P]) for i in range(2)]

        w_in = [st.sem(f"w_in{i}") for i in range(2)]
        b_in, b2_in = st.sem("b_in"), [st.sem(f"b2_in{i}") for i in range(2)]
        w1_hi_d, w1_lo_d, w2_hi_d, w2_lo_d = (st.sem(n) for n in ("w1_hi_d", "w1_lo_d", "w2_hi_d", "w2_lo_d"))
        rows_set, gathered = st.sem("rows_set"), [st.sem(f"gathered{i}") for i in range(2)]
        x_turned, x_hi, x_lo = st.sem("x_turned"), st.sem("x_hi"), st.sem("x_lo")
        h_done, h_val_d, h_hi_d, h_lo_d = (st.sem(n) for n in ("h_done", "h_val_d", "h_hi_d", "h_lo_d"))
        y_done, y_biased, y_ready = st.sem("y_done"), st.sem("y_biased"), st.sem("y_ready")
        scattered, passed = st.sem("scattered"), st.sem("passed")

        def experts(eng, program):
            with eng.Fori(0, E // 2 - 1) as i:
                for ep in range(2):
                    program(i * 2 + ep, ep, i, False)
            for ep in range(2):
                program(E - 2 + ep, ep, E // 2 - 1, True)

        def ahead(ep, last):
            return not (last and ep == 1)

        with nc.Block() as block:
            @block.sync
            def _(sp):
                def load(i, u):
                    e, q, par = i * 2 + u // NQD, u % NQD, u % 2
                    cols = slice(q * FQ * P, (q + 1) * FQ * P)
                    sp.dma_start(w1_raw[:, par], w1[bass.ds(e, 1), :, cols].rearrange("o (c p) n -> p (o c) n", p=P)
                                 ).then_inc(w_in[par], 16)
                    sp.dma_start(w2_raw[:, par], w2[bass.ds(e, 1), cols, :].rearrange("o (c p) n -> p (o c) n", p=P)
                                 ).then_inc(w_in[par], 16)

                sp.dma_start(b1[:], b1_cols).then_inc(b_in, 16)
                load(0, 0)
                load(0, 1)

                def program(e, ep, i, last):
                    for q in range(NQD):
                        u = ep * NQD + q
                        if not last or u + 2 < 2 * NQD:
                            sp.wait_ge(w1_lo_d, e * NQD + q + 1)
                            sp.wait_ge(w2_lo_d, e * NQD + q + 1)
                            load(i, u + 2)
                        if q == 0:
                            sp.wait_ge(y_biased, (i * 2) * NS)
                            sp.dma_start(b2_all[:, ep], b2[bass.ds(e, 1), :].rearrange("o d -> (o d)").partition_broadcast(NQ)
                                         ).then_inc(b2_in[ep], 16)

                experts(sp, program)

            @block.gpsimd
            def _(pool):
                def gather(e, par):
                    nc.gpsimd.tensor_copy(rows_now[:, par], slot_rows[:, bass.ds(e * NS, NS)]).then_inc(rows_set, 1)
                    wait_first(pool, rows_set, e + 1, passed)
                    for s in range(NS):
                        nc.gpsimd.indirect_dma_start(
                            out=xg[:, par, s], out_offset=None, in_=table,
                            in_offset=bass.IndirectOffsetOnAxis(ap=rows_now[:, par, s:s + 1], axis=0)
                        ).then_inc(gathered[par], 16)

                def w2_low(n, par):
                    pool.wait_ge(w2_hi_d, n + 1)
                    nc.gpsimd.tensor_tensor(w2_lo[:, par], w2_raw[:, par], f32(w2_hi[:, par]), ALU.subtract).then_inc(w2_lo_d, 1)

                gather(0, 0)
                w2_low(0, 0)

                def program(e, ep, i, last):
                    for q in range(NQD):
                        if q == 0 and ahead(ep, last):
                            gather(e + 1, 1 - ep)
                        if q < NQD - 1 or ahead(ep, last):
                            w2_low(e * NQD + q + 1, (ep * NQD + q + 1) % 2)
                    for s in range(NS):
                        wait_first(pool, y_ready, e * NS + s + 1, passed)
                        nc.gpsimd.indirect_dma_start(
                            out=acc, out_offset=bass.IndirectOffsetOnAxis(ap=rows_now[:, ep, s:s + 1], axis=0),
                            in_=y_val[:, s], in_offset=None, compute_op=ALU.add).then_inc(scattered, 16)
                    wait_first(pool, scattered, e * (16 * NS) + 16 * NS, passed)

                experts(pool, program)

            @block.scalar
            def _(act):
                def x_high(e, par):
                    for s in range(NS):
                        act.wait_ge(x_turned, e * NS + s + 1)
                        nc.scalar.activation(xe_hi[:, par, :, s * NQ:(s + 1) * NQ], xp[s % 2][:, :, 0:NQ],
                                             ACT.Copy).then_inc(x_hi, 1)

                def w_high(par, uses):
                    act.wait_ge(w_in[par], uses * 32)
                    nc.scalar.activation(w1_hi[:, par], w1_raw[:, par], ACT.Copy).then_inc(w1_hi_d, 1)
                    nc.scalar.activation(w2_hi[:, par], w2_raw[:, par], ACT.Copy).then_inc(w2_hi_d, 1)

                w_high(0, 1)
                x_high(0, 0)
                act.wait_ge(b_in, 16)

                def program(e, ep, i, last):
                    for q in range(NQD):
                        u = ep * NQD + q
                        for f in range(FQ):
                            m = (e * NQD + q) * FQ + f
                            act.wait_ge(h_done, m + 1)
                            nc.scalar.activation(h_val[:, f % 2], hp[f % 2][:], act_func,
                                                 bias=b1[:, bass.ds(m, 1)]).then_inc(h_val_d, 1)
                            if f == 1 and (q < NQD - 1 or ahead(ep, last)):
                                w_high((u + 1) % 2, i * NQD + (u + 1) // 2 + 1)
                        if q == NQD // 2 and ahead(ep, last):
                            x_high(e + 1, 1 - ep)

                experts(act, program)

            @block.vector
            def _(dve):
                def x_low(e, par):
                    for s in range(NS):
                        dve.wait_ge(x_hi, e * NS + s + 1)
                        cols = slice(s * NQ, (s + 1) * NQ)
                        nc.vector.tensor_tensor(xe_lo[:, par, :, cols], xp[s % 2][:, :, 0:NQ], f32(xe_hi[:, par, :, cols]),
                                                ALU.subtract).then_inc(x_lo, 1)

                def w1_low(n, par):
                    dve.wait_ge(w1_hi_d, n + 1)
                    nc.vector.tensor_tensor(w1_lo[:, par], w1_raw[:, par], f32(w1_hi[:, par]), ALU.subtract).then_inc(w1_lo_d, 1)

                w1_low(0, 0)
                x_low(0, 0)

                def program(e, ep, i, last):
                    for q in range(NQD):
                        for f in range(FQ):
                            m = (e * NQD + q) * FQ + f
                            dve.wait_ge(h_val_d, m + 1)
                            nc.vector.tensor_copy(h_hi[:, f % 2], h_val[:, f % 2]).then_inc(h_hi_d, 1)
                            dve.wait_ge(h_hi_d, m + 1)
                            nc.vector.tensor_tensor(h_lo[:, f % 2], h_val[:, f % 2], f32(h_hi[:, f % 2]),
                                                    ALU.subtract).then_inc(h_lo_d, 1)
                            if f == 1 and (q < NQD - 1 or ahead(ep, last)):
                                w1_low(e * NQD + q + 1, (ep * NQD + q + 1) % 2)
                        if q == NQD // 2 and ahead(ep, last):
                            x_low(e + 1, 1 - ep)
                    dve.wait_ge(b2_in[ep], i * 16 + 16)
                    dve.wait_ge(scattered, e * (16 * NS))
                    for s in range(NS):
                        dve.wait_ge(y_done, e * NS + s + 1)
                        nc.vector.tensor_tensor(y_val[:, s], yp[s][0:NQ, :], b2_all[:, ep], ALU.add).then_inc(y_biased, 1)
                    for s in range(NS):
                        dve.wait_ge(y_biased, e * NS + s + 1)
                        gate = xg[:, ep, s, bass.ds(e + D, 1)]
                        nc.vector.tensor_scalar(y_val[:, s], y_val[:, s], gate, None, ALU.mult).then_inc(y_ready, 1)

                experts(dve, program)

            @block.tensor
            def _(pe):
                def turn(e, par, gathers):
                    pe.wait_ge(gathered[par], gathers * (16 * NS))
                    for s in range(NS):
                        pe.wait_ge(x_lo, e * NS + max(s - 1, 0))
                        for c in range(DC):
                            last = nc.tensor.transpose(xp[s % 2][:, c, 0:NQ], xg[:, par, s, c * P:(c + 1) * P],
                                                       ident[0:NQ, 0:NQ])
                        last.then_inc(x_turned, 1)

                turn(0, 0, 1)

                def program(e, ep, i, last):
                    def second(q, f):
                        m = (e * NQD + q) * FQ + f
                        par = (ep * NQD + q) % 2
                        first, final = q == 0 and f == 0, q == NQD - 1 and f == FQ - 1
                        if f == 0:
                            pe.wait_ge(w2_lo_d, e * NQD + q + 1)
                        pe.wait_ge(h_lo_d, m + 1)
                        for s in range(NS):
                            if first:
                                pe.wait_ge(y_biased, e * NS)
                            rows = slice(s * NQ, (s + 1) * NQ)
                            ops = three_passes((h_hi[:, f % 2, rows], h_lo[:, f % 2, rows]), (w2_hi[:, par, f], w2_lo[:, par, f]))
                            for k, (w, mv) in enumerate(ops):
                                mm = nc.tensor.matmul(yp[s][0:NQ, :], w, mv, start=(first and k == 0), stop=(final and k == 2))
                            if final:
                                mm.then_inc(y_done, 1)

                    before = None
                    pe.wait_ge(x_lo, e * NS + NS)
                    for q in range(NQD):
                        par = (ep * NQD + q) % 2
                        pe.wait_ge(w1_lo_d, e * NQD + q + 1)
                        for f in range(FQ):
                            cols = slice(f * P, (f + 1) * P)
                            product(nc, hp[f % 2][:], [
                                ((w1_hi[:, par, c, cols], w1_lo[:, par, c, cols]), (xe_hi[:, ep, c], xe_lo[:, ep, c]))
                                for c in range(DC)]).then_inc(h_done, 1)
                            if before is not None:
                                second(*before)
                            before = (q, f)
                        if q == NQD // 2 and ahead(ep, last):
                            turn(e + 1, 1 - ep, i + 1 + ep)
                    second(*before)

                experts(pe, program)


def final_stage(nc, acc, out_rows):
    with ExitStack() as ctx:
        st = Stage(nc, ctx, "final")
        copied = st.sem("copied")
        with nc.Block() as block:
            @block.sync
            def _(sp):
                sp.dma_start(out_rows, acc[0:NT, :]).then_inc(copied, 16)
                sp.wait_ge(copied, 16)


def two_layers_kernel(nc, a, out):
    scratch = lambda name, shape, dt=F32: nc.dram_tensor(name, shape, dt).ap()
    with ExitStack() as ctx:
        ident = ctx.enter_context(nc.sbuf_tensor("ident", [P, P], F32))
        setup_stage(nc, ident)
        x_rows = a["x"].rearrange("b q d -> (b q) d")
        layers = [
            dict(n=0, inner=1024, heads=16, rows=x_rows, slots=400, choose="tokens", capacity=None, func=ACT.Gelu, gated=False),
            dict(n=1, inner=512, heads=16, slots=200, choose="expert", capacity=NT // E, func=ACT.Relu, gated=True),
        ]
        for layer in layers:
            n = layer["n"]
            T = layer["inner"] // P
            HP = P // (layer["inner"] // layer["heads"])
            g = lambda name: a[f"L{n}_{name}"]
            rows = layer["rows"] if n == 0 else layers[0]["acc"][0:NT, :]
            queries = scratch(f"queries{n}", (P, NB, T, 2, NQ))
            attended = scratch(f"attended{n}", (P, NB, T, NQ))
            acc = layer["acc"] = scratch(f"acc{n}", (ROWS, D))
            table = scratch(f"table{n}", (ROWS, TABLE_W))
            hd = layer["inner"] // layer["heads"]
            query_stage(nc, f"q{n}", ident, rows, g("wq"), g("bq"), float(np.float32(hd) ** np.float32(-0.5)), queries)
            for h in range(T // TT):
                cols = slice(h * TW, (h + 1) * TW)
                tiles = slice(h * TT, (h + 1) * TT)
                attention_pass(nc, f"a{n}{h}", ident, h * TT, HP, a["ctx_t"], g("wk")[:, cols], g("wv")[:, cols],
                               g("bk")[:, tiles], g("bv")[:, tiles], queries, attended)
            with ExitStack() as mid:
                slot_rows = mid.enter_context(nc.sbuf_tensor(f"slot_rows{n}", [NQ, (E + 1) * (layer["slots"] // NQ)], U32))
                with ExitStack() as short:
                    logits_t = short.enter_context(nc.sbuf_tensor(f"logits_t{n}", [P, NT], F32))
                    logits = short.enter_context(nc.sbuf_tensor(f"logits{n}", [NQ, NB, E], F32))
                    output_stage(nc, f"o{n}", ident, rows, g("wo"), g("bo"), attended, g("wg"), g("bg"), acc, table,
                                 logits_t, logits, layer["gated"])
                    route_stage(nc, f"r{n}", ident, logits_t, logits, layer["choose"], layer["slots"],
                                layer["capacity"], slot_rows)
                ffn_stage(nc, f"f{n}", ident, table, acc, slot_rows, g("w1"), g("b1"), g("w2"), g("b2"),
                          layer["slots"], layer["func"])
        final_stage(nc, layers[1]["acc"], out.rearrange("b q d -> (b q) d"))


def kernel(**inputs):
    import concourse.bacc as _bacc
    from concourse import mybir as _mybir
    from concourse.bass_utils import run_bass_kernel_spmd as _run

    i = {k: np.asarray(v) for k, v in inputs.items()}
    cols = lambda b: b.reshape(-1, P).T
    hidden = lambda b: b.reshape(E, -1, P).transpose(2, 0, 1).reshape(P, -1)
    repeat = lambda w: np.tile(w, (1, REP))
    ctx_t = i["ctx_1024"].transpose(0, 2, 1)
    laid = {
        "x": i["x"],
        "ctx_t": np.concatenate([ctx_t, np.zeros((NB, D, NKP - NK), ctx_t.dtype)], axis=2),
        "L0_wq": i["L0_xattn_Wq"].T, "L0_bq": cols(i["L0_xattn_bq"]),
        "L0_wk": i["L0_xattn_Wk"].T, "L0_bk": cols(i["L0_xattn_bk"]),
        "L0_wv": i["L0_xattn_Wv"].T, "L0_bv": cols(i["L0_xattn_bv"]),
        "L0_wo": i["L0_xattn_Wo"].T, "L0_bo": i["L0_xattn_bo"],
        "L0_wg": repeat(i["L0_ffn_Wg"]), "L0_bg": np.zeros((P, 1), np.float32),
        "L0_w1": i["L0_ffn_W1"], "L0_b1": hidden(i["L0_ffn_b1"]), "L0_w2": i["L0_ffn_W2"], "L0_b2": i["L0_ffn_b2"],
        "L1_wq": i["L1_xattn_Wq"], "L1_bq": cols(i["L1_xattn_bq"]),
        "L1_wk": i["L1_xattn_Wkv"][:, 0:D], "L1_bk": cols(i["L1_xattn_bkv"][0:D]),
        "L1_wv": i["L1_xattn_Wkv"][:, D:2 * D], "L1_bv": cols(i["L1_xattn_bkv"][D:2 * D]),
        "L1_wo": i["L1_xattn_Wproj"], "L1_bo": i["L1_xattn_bproj"],
        "L1_wg": repeat(i["L1_ffn_Wr"]), "L1_bg": np.tile(i["L1_ffn_br"], REP).reshape(P, 1),
        "L1_w1": i["L1_ffn_W1"], "L1_b1": hidden(i["L1_ffn_b1"]), "L1_w2": i["L1_ffn_W2"], "L1_b2": i["L1_ffn_b2"],
    }
    nc = _bacc.Bacc("TRN2", target_bir_lowering=False, num_devices=1)
    arrays, args = {}, {}
    for name, value in laid.items():
        arrays[f"in_{name}"] = value = np.ascontiguousarray(value)
        args[name] = nc.dram_tensor(f"in_{name}", value.shape, _mybir.dt.from_np(value.dtype), kind="ExternalInput").ap()
    out = nc.dram_tensor("out", (NB, NQ, D), F32, kind="ExternalOutput").ap()
    two_layers_kernel(nc, args, out)
    r = _run(nc, [arrays], core_ids=[0])
    return r.results[0]["out"]
```

```python
from contextlib import ExitStack

import concourse.bass as bass
from concourse import mybir
import numpy as np

F32 = mybir.dt.float32
F32R = mybir.dt.float32r
F16 = mybir.dt.float16
BF16 = mybir.dt.bfloat16
I32 = mybir.dt.int32
U32 = mybir.dt.uint32
ALU = mybir.AluOpType
ACT = mybir.ActivationFunctionType
AX_X = mybir.AxisListType.X

P = 128
NB = 16
NQ = 100
NT = NB * NQ
NK = 722
D = 512
DC = D // P
KT = 6
KR = 121
NKP = KT * KR
KA = 362
KH = NK // 2
KPAD = 724
TW = 512
TT = TW // P
E = 8
REP = P // E
EPS = 1e-5
SLOT_MAX = 200
ROWS = NT + SLOT_MAX
TABLE_W = D + E


def f32(ap):
    return ap.bitcast(F32)


def three_passes(hi_lo_w, hi_lo_m):
    (w_hi, w_lo), (m_hi, m_lo) = hi_lo_w, hi_lo_m
    return [(w_lo, m_hi), (w_hi, m_lo), (w_hi, m_hi)]


def product(nc, out, chunks, first=True, final=True):
    todo = [p for c in chunks for p in three_passes(*c)]
    for n, (w, m) in enumerate(todo):
        last = nc.tensor.matmul(out, w, m, start=(first and n == 0), stop=(final and n == len(todo) - 1))
    return last


class Chain:

    def __init__(self, eng, sem, start=0):
        self.eng, self.sem, self.start, self.n = eng, sem, start, 0

    def step(self, ins):
        self.n += 1
        ins.then_inc(self.sem, 1)

    def wait(self):
        self.eng.wait_ge(self.sem, self.start + self.n)

    def link(self, ins):
        self.step(ins)
        self.wait()


def wait_first(eng, sem, value, passed):
    eng.wait_ge(sem, value)
    eng.sem_inc(passed, 1)


class Stage:

    def __init__(self, nc, ctx, tag):
        self.nc, self.ctx, self.tag = nc, ctx, tag
        self.sems = []
        ctx.callback(self.clear)

    def clear(self):
        if self.sems:
            self.nc.clear_and_free_semaphores(self.sems)
            self.nc.all_engine_barrier()

    def sb(self, name, shape, dt):
        return self.ctx.enter_context(self.nc.sbuf_tensor(f"{self.tag}_{name}", shape, dt))

    def ps(self, name, shape, dt=F32):
        return self.ctx.enter_context(self.nc.psum_tensor(f"{self.tag}_{name}", shape, dt))

    def sem(self, name):
        self.sems.append(self.nc.alloc_semaphore(f"{self.tag}_{name}"))
        return self.sems[-1]


def row_stats(nc, stats, x_all, b):
    return nc.vector.bn_stats(stats[:, bass.ds(b, 1)].rearrange("p o s -> p (o s)"),
                              x_all[:, bass.ds(b, 1)].rearrange("p o d -> p (o d)"))


def layernorm_scales(nc, dve, chain, bufs, var_ready, std_ready):
    stats, moments, veps, std, rstd, tmp = bufs
    for b in range(NB):
        ins = nc.vector.bn_aggr(moments[:, b, :], stats[:, b, :])
    chain.link(ins)
    nc.vector.tensor_scalar(veps[:], moments[:, :, 1], EPS, None, ALU.add).then_inc(var_ready, 1)
    dve.wait_ge(std_ready, 1)
    chain.link(nc.vector.reciprocal(rstd[:], std[:]))
    chain.link(nc.vector.tensor_tensor(tmp[:], rstd[:], rstd[:], ALU.mult))
    chain.link(nc.vector.tensor_tensor(tmp[:], tmp[:], veps[:], ALU.mult))
    chain.link(nc.vector.tensor_scalar(tmp[:], tmp[:], -0.5, 1.5, ALU.mult, ALU.add))
    chain.link(nc.vector.tensor_tensor(rstd[:], rstd[:], tmp[:], ALU.mult))


def layernorm_buffers(st):
    return (st.sb("stats", [NQ, NB, 6], F32), st.sb("moments", [NQ, NB, 2], F32), st.sb("veps", [NQ, NB], F32),
            st.sb("std", [NQ, NB], F32), st.sb("rstd", [NQ, NB], F32), st.sb("newton", [NQ, NB], F32))


def setup_stage(nc, ident):
    with ExitStack() as ctx:
        st = Stage(nc, ctx, "setup")
        zeroed = st.sem("zeroed")
        made = st.sem("made")
        with nc.Block() as block:
            @block.gpsimd
            def _(pool):
                nc.gpsimd.memset(ident[:], 0.0).then_inc(zeroed, 1)
                pool.wait_ge(zeroed, 1)
                nc.gpsimd.affine_select(out=ident[:], in_=ident[:], compare_op=ALU.not_equal, fill=1.0, base=0,
                                        pattern=[[-1, P]], channel_multiplier=1).then_inc(made, 1)
                pool.wait_ge(made, 1)


def query_stage(nc, tag, ident, x_rows, wq_t, bq_cols, scale, queries):
    T = wq_t.shape[1] // P
    CG = 4
    NG = NB // CG
    with ExitStack() as ctx:
        st = Stage(nc, ctx, tag)
        x_all = st.sb("x", [NQ, NB, D], F32)
        ln = layernorm_buffers(st)
        stats, moments, veps, std, rstd, _ = ln
        xt_hi = st.sb("xt_hi", [P, DC, NT], F32R)
        xt_lo = st.sb("xt_lo", [P, DC, NT], F32R)
        w_raw = st.sb("w_raw", [P, DC, T * P], F32)
        w_hi = st.sb("w_hi", [P, DC, T * P], F32R)
        w_lo = st.sb("w_lo", [P, DC, T * P], F32R)
        bias = st.sb("bias", [P, T], F32)
        bias_s = st.sb("bias_s", [P, T], F32)
        q_val = st.sb("q_val", [P, 2, CG * NQ], F32)
        q_out = st.sb("q_out", [P, 2, CG, 2, NQ], F32R)
        xp = [st.ps(f"xp{i}", [P, DC, P]) for i in range(2)]
        qp = [st.ps(f"qp{i}", [P, CG * NQ]) for i in range(4)]

        x_in, w_in, b_in = [st.sem(f"x_in{g}") for g in range(NG)], st.sem("w_in"), st.sem("b_in")
        var_ready, std_ready, step = st.sem("var_ready"), st.sem("std_ready"), st.sem("step")
        xn_ready, xt_done, xt_hi_done, xt_lo_done = (st.sem(n) for n in ("xn_ready", "xt_done", "xt_hi_done", "xt_lo_done"))
        w_hi_done, w_lo_done, bias_done = st.sem("w_hi_done"), st.sem("w_lo_done"), st.sem("bias_done")
        q_done, q_val_done, q_hi_done, q_lo_done = (st.sem(n) for n in ("q_done", "q_val_done", "q_hi_done", "q_lo_done"))
        q_stored = [st.sem(f"q_stored{i}") for i in range(2)]

        with nc.Block() as block:
            @block.sync
            def _(sp):
                for g in range(NG):
                    sp.dma_start(x_all[:, g * CG:(g + 1) * CG], x_rows.rearrange("(b p) d -> p b d", p=NQ)[:, g * CG:(g + 1) * CG]
                                 ).then_inc(x_in[g], 16)
                sp.dma_start(w_raw[:], wq_t.rearrange("(c p) n -> p c n", p=P)).then_inc(w_in, 16)
                sp.dma_start(bias[:], bq_cols).then_inc(b_in, 16)
                with sp.Fori(0, NG) as g:
                    for t in range(T):
                        sp.wait_ge(q_lo_done, g * T + t + 1)
                        sp.dma_start(queries[:, bass.ds(g * CG, CG), t], f32(q_out[:, t % 2])).then_inc(q_stored[t % 2], 16)
                for i in range(2):
                    sp.wait_ge(q_stored[i], 16 * NG * T // 2)

            @block.gpsimd
            def _(pool):
                pool.wait_ge(w_hi_done, 1)
                nc.gpsimd.tensor_tensor(w_lo[:], w_raw[:], f32(w_hi[:]), ALU.subtract).then_inc(w_lo_done, 1)

            @block.vector
            def _(dve):
                def split_low(b):
                    dve.wait_ge(xt_hi_done, b + 1)
                    cols = slice(b * NQ, (b + 1) * NQ)
                    nc.vector.tensor_tensor(xt_lo[:, :, cols], xp[b % 2][:, :, 0:NQ], f32(xt_hi[:, :, cols]),
                                            ALU.subtract).then_inc(xt_lo_done, 1)

                chain = Chain(dve, step)
                for b in range(NB):
                    if b % CG == 0:
                        dve.wait_ge(x_in[b // CG], 16)
                    ins = row_stats(nc, stats, x_all, b)
                chain.link(ins)
                layernorm_scales(nc, dve, chain, ln, var_ready, std_ready)
                for b in range(NB):
                    nc.vector.tensor_scalar(x_all[:, b, :], x_all[:, b, :], moments[:, b, 0:1], rstd[:, b:b + 1],
                                            ALU.subtract, ALU.mult).then_inc(xn_ready, 1)
                    if b:
                        split_low(b - 1)
                split_low(NB - 1)
                dve.wait_ge(b_in, 16)
                nc.vector.tensor_scalar(bias_s[:], bias[:], scale, None, ALU.mult).then_inc(bias_done, 1)
                with dve.Fori(0, NG) as g:
                    for t in range(T):
                        n = g * T + t
                        dve.wait_ge(q_val_done, n + 1)
                        dve.wait_ge(q_stored[t % 2], (g * T + t - t % 2) * 8)
                        val = q_val[:, t % 2].rearrange("p (b q) -> p b q", b=CG)
                        nc.vector.tensor_copy(q_out[:, t % 2, :, 0, :], val).then_inc(q_hi_done, 1)
                        dve.wait_ge(q_hi_done, n + 1)
                        nc.vector.tensor_tensor(q_out[:, t % 2, :, 1, :], val, f32(q_out[:, t % 2, :, 0, :]),
                                                ALU.subtract).then_inc(q_lo_done, 1)

            @block.scalar
            def _(act):
                act.wait_ge(w_in, 16)
                nc.scalar.activation(w_hi[:], w_raw[:], ACT.Copy).then_inc(w_hi_done, 1)
                act.wait_ge(var_ready, 1)
                nc.scalar.activation(std[:], veps[:], ACT.Sqrt).then_inc(std_ready, 1)
                for b in range(NB):
                    act.wait_ge(xt_done, b + 1)
                    nc.scalar.activation(xt_hi[:, :, b * NQ:(b + 1) * NQ], xp[b % 2][:, :, 0:NQ],
                                         ACT.Copy).then_inc(xt_hi_done, 1)
                act.wait_ge(bias_done, 1)
                with act.Fori(0, NG) as g:
                    for t in range(T):
                        n = g * T + t
                        act.wait_ge(q_done, n + 1)
                        if t >= 2:
                            act.wait_ge(q_lo_done, n - 1)
                        else:
                            act.wait_ge(q_lo_done, g * T)
                        nc.scalar.activation(q_val[:, t % 2], qp[t % 4][:], ACT.Identity, bias=bias_s[:, t:t + 1],
                                             scale=scale).then_inc(q_val_done, 1)

            @block.tensor
            def _(pe):
                for b in range(NB):
                    pe.wait_ge(xn_ready, b + 1)
                    if b >= 2:
                        pe.wait_ge(xt_lo_done, b - 1)
                    for c in range(DC):
                        last = nc.tensor.transpose(xp[b % 2][:, c, 0:NQ], x_all[:, b, c * P:(c + 1) * P],
                                                   ident[0:NQ, 0:NQ])
                    last.then_inc(xt_done, 1)
                pe.wait_ge(xt_lo_done, NB)
                pe.wait_ge(w_lo_done, 1)
                with pe.Fori(0, NG) as g:
                    cols = bass.ds(g * (CG * NQ), CG * NQ)
                    for t in range(T):
                        if t >= 4:
                            pe.wait_ge(q_val_done, g * T + t - 3)
                        else:
                            pe.wait_ge(q_val_done, g * T)
                        product(nc, qp[t % 4][:], [
                            ((w_hi[:, c, t * P:(t + 1) * P], w_lo[:, c, t * P:(t + 1) * P]),
                             (xt_hi[:, c, cols], xt_lo[:, c, cols])) for c in range(DC)]).then_inc(q_done, 1)


def assign_banks(plan, banks):
    starts = [(u, k) for k, slot in enumerate(plan) for u, begin, _ in slot if begin == 0]
    ends = {u: k for k, slot in enumerate(plan) for u, _, end in slot if end == DC}
    ended = list(ends)

    def search(n, users, apart):
        if n == len(starts):
            fits = all(u and starts_at[u[0]] + len(plan) - ends[u[-1]] >= apart for u in users)
            return {u: bank for bank, own in enumerate(users) for u in own} if fits else None
        u, k = starts[n]
        for bank in sorted(range(banks), key=lambda i: ended.index(users[i][-1]) if users[i] else i - banks):
            if not users[bank] or k - ends[users[bank][-1]] >= apart:
                found = search(n + 1, [own + [u] if i == bank else own for i, own in enumerate(users)], apart)
                if found:
                    return found
        return None

    starts_at = dict(starts)
    return next(found for apart in (2, 0) if (found := search(0, [[]] * banks, apart)))


def attention_pass(nc, tag, ident, first_tile, HP, ctx_t, wk_t, wv_t, bk_cols, bv_cols, queries, attended):
    HD = P // HP
    NH = TT * HP
    K = lambda t, h, rel: ("k", t, h, rel)
    V = lambda j: ("v", j, 0, 1)
    if NH == 8:
        plan = [[K(3, 0, 0), K(3, 1, 0)], [V(0)], [K(0, 0, 1), K(0, 1, 1)], [V(1), V(2)],
                [K(1, 0, 1), K(1, 1, 1)], [V(3)], [K(2, 0, 1), K(2, 1, 1)], [V(4), V(5)]]
    else:
        plan = [[K(3, 0, 0)], [K(3, 1, 0)], [(V(0), 0, 3)], [(V(0), 3, 4), (V(1), 0, 2)],
                [K(0, 0, 1)], [K(0, 1, 1)], [(V(1), 2, 4), (V(2), 0, 1)], [(V(2), 1, 4)],
                [K(1, 0, 1)], [K(1, 1, 1)], [(V(3), 0, 3)], [(V(3), 3, 4), (V(4), 0, 2)],
                [K(2, 0, 1)], [K(2, 1, 1)], [(V(4), 2, 4), (V(5), 0, 1)], [(V(5), 1, 4)]]
    plan = [[part if len(part) == 3 else (part, 0, DC) for part in slot] for slot in plan]
    parts = [part for slot in plan for part in slot]
    order = [u for u, _, end in parts if end == DC]
    UN = len(order)
    BANKS = 3
    DEFER = NH > 8
    bank_of = assign_banks(plan, BANKS)
    starts = [u for u, begin, _ in parts if begin == 0]

    def slot_count(b, u):
        return (b + 1) * UN + (order.index(u) - 1)

    def unit_count(b, u):
        return slot_count(b - u[3], u)

    def bank_free(b, u):
        n = starts.index(u)
        same = [v for v in starts[n + 1:] + starts[:n + 1] if bank_of[v] == bank_of[u]]
        v = same[-2] if len(same) > 1 else u
        return slot_count(b, v) - (0 if starts.index(v) < n else UN)

    with ExitStack() as ctx:
        st = Stage(nc, ctx, tag)
        wk_hi, wk_lo, wv_hi, wv_lo = (st.sb(n, [P, DC, TW], F32R) for n in ("wk_hi", "wk_lo", "wv_hi", "wv_lo"))
        c_raw = st.sb("c_raw", [P, DC, NKP], F32)
        c_hi = st.sb("c_hi", [P, 2, DC, NKP], F32R)
        c_lo = st.sb("c_lo", [P, 2, DC, NKP], F32R)
        kx = st.sb("kx", [P, 2 * TT, KPAD], F32R)
        k_low = st.sb("k_low", [P, 2, KA], F32R)
        v_hi = st.sb("v_hi", [KR, 2, KT, TW], F32R)
        v_lo = st.sb("v_lo", [KR, 2, KT, TW], F32R)
        q_in = st.sb("q_in", [P, NH, 2, NQ], F32R)
        work = st.sb("work", [P, 4 * TW], F32)
        w_raw = work[:, :].rearrange("p (c n) -> p c n", c=DC)
        probs = work[0:NQ, 0:2 * NKP].rearrange("p (a n) -> p a n", a=2)
        pt = st.sb("pt", [KR, KT, 2, HP, NQ], F32R)
        pt_hi, pt_lo = pt[:, :, 0], pt[:, :, 1]
        BOTH = 2 * HP * NQ <= 512
        pv_rest = st.sb("pv_rest", [P, HP * NQ], F32) if BOTH else None
        o_t = st.sb("o_t", [P, 2, TT, NQ], F32)
        bk = st.sb("bk", [P, TT], F32)
        bv = st.sb("bv", [P, TT], F32)
        neg_max = st.sb("neg_max", [NQ, 2], F32)
        row_sum = st.sb("row_sum", [NQ, 2], F32)
        row_inv = st.sb("row_inv", [NQ, 2], F32)

        sc = st.ps("sc", [P, 2, 512])
        up_all = st.ps("up", [P, BANKS, 512])
        up = [up_all[:, i] for i in range(BANKS)]
        tp = st.ps("tp", [P, 2, 512])
        pv = st.ps("pv", [P, 512])

        w_in, w_hi_done, w_lo_done = st.sem("w_in"), st.sem("w_hi_done"), st.sem("w_lo_done")
        b_in, zeroed = st.sem("b_in"), st.sem("zeroed")
        ctx_in, ctx_hi_done, ctx_split = st.sem("ctx_in"), st.sem("ctx_hi_done"), st.sem("ctx_split")
        unit_done, unit_hi, unit_lo = st.sem("unit_done"), st.sem("unit_hi"), st.sem("unit_lo")
        q_loaded = [st.sem(f"q_loaded{t}") for t in range(TT)]
        k_moved = [st.sem(f"k_moved{t}") for t in range(TT)]
        s_done, max_done, exp_done, inv_done, p_done = (st.sem(n) for n in ("s_done", "max_done", "exp_done", "inv_done", "p_done"))
        t_done, t_hi, t_lo = st.sem("t_done"), st.sem("t_hi"), st.sem("t_lo")
        pv_done, rest_done, o_done = st.sem("pv_done"), st.sem("rest_done"), st.sem("o_done")
        o_stored = [st.sem(f"o_stored{i}") for i in range(2)]
        passed = st.sem("passed")

        def head(b, k):
            return b * NH + k

        def group(b, t):
            return b * TT + t

        def slots(b, par, last):
            first = isinstance(b, int) and b == 0
            for k in range(NH):
                yield ("scores", k)
                if k > 0:
                    yield ("turn", b, k - 1)
                elif not first:
                    yield ("turn", b - 1, NH - 1)
                if DEFER and k > 0:
                    for u, _, end in plan[k - 1]:
                        if end == DC and not (last and u[3]):
                            yield ("evacuate", b, par, u)
                elif DEFER and not first:
                    for u, _, end in plan[NH - 1]:
                        if end == DC:
                            yield ("evacuate", b - 1, 1 - par, u)
                for part in plan[k]:
                    if not (last and part[0][3]):
                        yield ("unit", *part)
                        if part[2] == DC and not DEFER:
                            yield ("evacuate", b, par, part[0])
                if k % HP == 0 and (k > 0 or not first):
                    yield ("values", b if k else b - 1, (k // HP - 1) % TT)
            if last:
                yield ("turn", b, NH - 1)
                yield ("values", b, TT - 1)

        def rows_of(j):
            return slice(j * HD, (j + 1) * HD)

        def moved(n):
            return n * (32 * HP)

        first_odd = next(k for k in range(1, NH, 2) if any(part[0] == K(3, 1, 0) for slot in plan[:k - DEFER] for part in slot))

        def scores_at(k, last):
            return up_all[:, 0:2] if last and k % 2 and k >= first_odd else sc

        def reorder(steps):
            out = []
            for s in steps:
                if s[0] == "turn" and out and out[-1][0] == "scores" and s[2] != out[-1][1]:
                    out.insert(len(out) - 1, s)
                else:
                    out.append(s)
            return out

        def batches(eng, program, peeled=1):
            pairs = (NB - 1 - peeled) // 2
            program(0, 0, False, 0)
            with eng.Fori(0, pairs) as i:
                program(i * 2 + 1, 1, False, i)
                program(i * 2 + 2, 0, False, i + 1)
            for b in range(2 * pairs + 1, NB):
                program(b, b % 2, b == NB - 1, b // 2)

        with nc.Block() as block:
            @block.sync
            def _(sp):
                def load_ctx(b):
                    sp.dma_start(c_raw[:], ctx_t[bass.ds(b, 1)].rearrange("o (c p) k -> p (o c) k", p=P)).then_inc(ctx_in, 16)

                def load_q(b, t):
                    for j in range(HP):
                        for r in (j, j ^ 1):
                            sp.dma_start(f32(q_in[rows_of(r), t * HP + j]),
                                         queries[rows_of(j), bass.ds(b, 1), first_tile + t].rearrange("p o a q -> p (o a) q")
                                         ).then_inc(q_loaded[t], 16)

                def move_low(count, u):
                    _, t, half, _ = u
                    lo, n = (0, KA) if half == 0 else (KA, NK - KA)
                    sp.wait_ge(unit_lo, count)
                    for j in range(HP):
                        sp.dma_start(f32(kx[rows_of(j ^ 1), 2 * t + j % 2, lo:lo + n]),
                                     f32(k_low[rows_of(j), half, 0:n])).then_inc(k_moved[t], 16)

                sp.dma_start(w_raw, wk_t.rearrange("(c p) n -> p c n", p=P)).then_inc(w_in, 16)
                load_ctx(0)
                sp.dma_start(bk[:], bk_cols).then_inc(b_in, 16)
                sp.dma_start(bv[:], bv_cols).then_inc(b_in, 16)
                sp.wait_ge(zeroed, 1)
                sp.wait_ge(w_hi_done, 1)
                sp.wait_ge(w_lo_done, 1)
                sp.dma_start(w_raw, wv_t.rearrange("(c p) n -> p c n", p=P)).then_inc(w_in, 16)
                for t in range(TT):
                    load_q(0, t)
                sp.wait_ge(ctx_split, 1)
                load_ctx(1)
                for u in order:
                    if u[3] and u[0] == "k":
                        move_low(slot_count(-1, u), u)

                def program(b, par, last, half_b):
                    if not isinstance(b, int) or b + 2 < NB:
                        sp.wait_ge(ctx_split, b + 2)
                        load_ctx(b + 2)
                    for s in slots(b, par, last):
                        if s[0] == "scores" and s[1] % HP == HP - 1 and not last:
                            sp.wait_ge(s_done, head(b, s[1]) + 1)
                            load_q(b + 1, s[1] // HP)
                        elif s[0] == "evacuate" and s[3][0] == "k":
                            move_low(slot_count(s[1], s[3]), s[3])
                        elif s[0] == "values" and s[2] == TT - 1:
                            vb, vp = s[1], par if s[1] is b else 1 - par
                            sp.wait_ge(o_done, group(vb, TT - 1) + 1)
                            sp.dma_start(attended[:, bass.ds(vb, 1), first_tile:first_tile + TT].rearrange("p o t q -> p (o t) q"),
                                         o_t[:, vp]).then_inc(o_stored[vp], 16)

                batches(sp, program, peeled=3)
                for par in range(2):
                    sp.wait_ge(o_stored[par], 16 * NB // 2)

            @block.gpsimd
            def _(pool):
                def split_ctx(b, par):
                    wait_first(pool, ctx_in, b * 16 + 16, passed)
                    nc.gpsimd.tensor_copy(c_hi[:, par], c_raw[:]).then_inc(ctx_hi_done, 1)
                    pool.wait_ge(ctx_hi_done, b + 1)
                    nc.gpsimd.tensor_tensor(c_lo[:, par], c_raw[:], f32(c_hi[:, par]), ALU.subtract).then_inc(ctx_split, 1)

                split_ctx(1, 1)
                with pool.Fori(1, NB // 2) as i:
                    for par in range(2):
                        b = i * 2 + par
                        pool.wait_ge(unit_done, slot_count(b - 2, K(3, 1, 0)))
                        split_ctx(b, par)

            @block.tensor
            def _(pe):
                def unit(b, u, wait_bank=None, begin=0, end=DC):
                    kind, t, half, rel = u
                    par = (par_of[0] + rel) % 2
                    chunks = range(begin, end)
                    if wait_bank is not None:
                        pe.wait_ge(unit_lo, wait_bank)
                    out = up[bank_of[u]]
                    if kind == "k":
                        lo, n = (0, KA) if half == 0 else (KA, NK - KA)
                        w = slice(t * P, (t + 1) * P)
                        last = product(nc, out[:, 0:n], [
                            ((wk_hi[:, c, w], wk_lo[:, c, w]), (c_hi[:, par, c, lo:lo + n], c_lo[:, par, c, lo:lo + n]))
                            for c in chunks], first=begin == 0, final=end == DC)
                    else:
                        r = slice(t * KR, (t + 1) * KR)
                        last = product(nc, out[0:KR, :], [
                            ((c_hi[:, par, c, r], c_lo[:, par, c, r]), (wv_hi[:, c, :], wv_lo[:, c, :]))
                            for c in chunks], first=begin == 0, final=end == DC)
                    if end == DC:
                        last.then_inc(unit_done, 1)

                par_of = [1]
                pe.wait_ge(w_hi_done, 1)
                pe.wait_ge(w_lo_done, 1)
                pe.wait_ge(ctx_split, 1)
                seen_v = False
                for n, u in enumerate(sorted((u for u in order if u[3]), key=order.index)):
                    if u[0] == "v" and not seen_v:
                        seen_v = True
                        pe.wait_ge(w_hi_done, 2)
                        pe.wait_ge(w_lo_done, 2)
                    free = bank_free(-1, u)
                    unit(-1, u, free if free > 0 else None)

                def program(b, par, last, half_b):
                    par_of[0] = par
                    for s in slots(b, par, last):
                        if s[0] == "scores":
                            k = s[1]
                            t = k // HP
                            g = head(b, k)
                            if k % HP == 0:
                                pe.wait_ge(q_loaded[t], (b + 1) * 32 * HP)
                                pe.wait_ge(k_moved[t], moved(b + 1))
                            if last and k == first_odd:
                                pe.wait_ge(unit_lo, slot_count(b, K(3, 1, 0)))
                            else:
                                pe.wait_ge(exp_done, g - 1 if last and k > first_odd else g)
                            for half in range(2):
                                keys = slice(half * KH, half * KH + KA)
                                for part in (1, 0):
                                    last_mm = nc.tensor.matmul(scores_at(k, last)[0:NQ, half, 0:KA], q_in[:, k, part],
                                                               kx[:, 2 * t + k % 2, keys], start=(part == 1), stop=(part == 0))
                            last_mm.then_inc(s_done, 1)
                        elif s[0] == "turn":
                            g = head(s[1], s[2])
                            pe.wait_ge(p_done, g + 1)
                            pe.wait_ge(t_lo, g)
                            for j in range(KT):
                                mm = nc.tensor.transpose(tp[0:KR, j // 3, (j % 3) * NQ:(j % 3 + 1) * NQ],
                                                         probs[:, s[2] % 2, j * KR:(j + 1) * KR], ident[0:NQ, 0:NQ])
                            mm.then_inc(t_done, 1)
                        elif s[0] == "unit":
                            u, begin, end = s[1:]
                            if u[0] == "v" and u[1] == 0 or u == K(0, 0, 1):
                                pe.wait_ge(ctx_split, b + 2)
                            unit(b, u, bank_free(b, u) if begin == 0 else None, begin, end)
                        elif s[0] == "values":
                            _, vb, t = s
                            vp = par if vb is b else 1 - par
                            cols = slice(t * P, (t + 1) * P)
                            pe.wait_ge(t_lo, head(vb, (t + 1) * HP - 1) + 1)
                            if t == 0:
                                pe.wait_ge(unit_lo, unit_count(vb, V(5)))
                            pe.wait_ge(o_done, group(vb, t))
                            if BOTH:
                                both, upper = pv[:, 0:2 * HP * NQ], pv[:, 0:HP * NQ]
                                for j in range(KT):
                                    todo = [(both, v_hi, pt[:, j]), (upper, v_lo, pt_hi[:, j])]
                                    for out, w, moving in reversed(todo) if j == KT - 1 else todo:
                                        mm = nc.tensor.matmul(out, w[:, vp, j, cols], moving, start=(j == 0 and out is both),
                                                              stop=(j == KT - 1 and out is both))
                                mm.then_inc(pv_done, 1)
                            else:
                                product(nc, pv[:, 0:HP * NQ], [
                                    ((v_hi[:, vp, j, cols], v_lo[:, vp, j, cols]), (pt_hi[:, j], pt_lo[:, j]))
                                    for j in range(KT)]).then_inc(pv_done, 1)

                batches(pe, program)

            @block.scalar
            def _(act):
                act.wait_ge(w_in, 16)
                nc.scalar.activation(wk_hi[:], w_raw, ACT.Copy).then_inc(w_hi_done, 1)
                act.wait_ge(ctx_in, 16)
                nc.scalar.activation(c_hi[:, 0], c_raw[:], ACT.Copy).then_inc(ctx_hi_done, 1)
                act.wait_ge(w_in, 32)
                nc.scalar.activation(wv_hi[:], w_raw, ACT.Copy).then_inc(w_hi_done, 1)
                act.wait_ge(b_in, 32)

                def unit(count, u, par):
                    kind, t, half, rel = u
                    act.wait_ge(unit_done, count)
                    if kind == "k":
                        lo, n = (0, KA) if half == 0 else (KA, NK - KA)
                        for odd in range(2):
                            ins = nc.scalar.activation(kx[:, 2 * t + odd, lo:lo + n], up[bank_of[u]][:, 0:n],
                                                       ACT.Identity, bias=bk[:, t:t + 1])
                    else:
                        ins = nc.scalar.activation(v_hi[:, (par + rel) % 2, t], up[bank_of[u]][0:KR, :], ACT.Copy)
                    ins.then_inc(unit_hi, 1)

                for u in order:
                    if u[3]:
                        unit(slot_count(-1, u), u, 1)

                def program(b, par, last, half_b):
                    steps = list(slots(b, par, last))
                    for s in reorder(steps):
                        if s[0] == "scores":
                            k = s[1]
                            g = head(b, k)
                            act.wait_ge(max_done, g + 1)
                            nc.scalar.activation(probs[:, k % 2, 0:NK].rearrange("p (a n) -> p a n", a=2),
                                                 scores_at(k, last)[0:NQ, :, 0:KH], ACT.Exp, bias=neg_max[:, k % 2:k % 2 + 1],
                                                 accum_out=row_sum[:, k % 2:k % 2 + 1]).then_inc(exp_done, 1)
                        elif s[0] == "turn":
                            g = head(s[1], s[2])
                            act.wait_ge(t_done, g + 1)
                            nc.scalar.activation(pt_hi[:, :, s[2] % HP, :].rearrange("p (a j) q -> p a j q", a=2),
                                                 tp[0:KR, :, 0:3 * NQ].rearrange("p a (j q) -> p a j q", j=3),
                                                 ACT.Copy).then_inc(t_hi, 1)
                        elif s[0] == "evacuate":
                            unit(slot_count(s[1], s[3]), s[3], s[2])
                        elif s[0] == "values" and BOTH:
                            act.wait_ge(pv_done, group(s[1], s[2]) + 1)
                            nc.scalar.activation(pv_rest[:], pv[:, HP * NQ:2 * HP * NQ], ACT.Identity,
                                                 bias=bv[:, s[2]:s[2] + 1]).then_inc(rest_done, 1)

                batches(act, program)

            @block.vector
            def _(dve):
                nc.vector.memset(f32(q_in[:]), 0.0)
                nc.vector.memset(f32(kx[:, :, NK:KPAD]), 0.0).then_inc(zeroed, 1)
                dve.wait_ge(w_hi_done, 1)
                nc.vector.tensor_tensor(wk_lo[:], w_raw, f32(wk_hi[:]), ALU.subtract).then_inc(w_lo_done, 1)
                dve.wait_ge(ctx_hi_done, 1)
                nc.vector.tensor_tensor(c_lo[:, 0], c_raw[:], f32(c_hi[:, 0]), ALU.subtract).then_inc(ctx_split, 1)
                dve.wait_ge(w_hi_done, 2)
                nc.vector.tensor_tensor(wv_lo[:], w_raw, f32(wv_hi[:]), ALU.subtract).then_inc(w_lo_done, 1)
                dve.wait_ge(w_lo_done, 2)
                nc.vector.memset(probs[:, :, NK:NKP], 0.0).then_inc(zeroed, 1)
                dve.wait_ge(b_in, 32)

                def unit(b, u, par):
                    kind, t, half, rel = u
                    dve.wait_ge(unit_hi, slot_count(b, u))
                    if kind == "k":
                        lo, n = (0, KA) if half == 0 else (KA, NK - KA)
                        before = b + rel if t == 0 else b + rel + 1
                        if not isinstance(before, int) or before > 0:
                            dve.wait_ge(k_moved[(t - 1) % TT], moved(before))
                        ins = nc.vector.scalar_tensor_tensor(out=k_low[:, half, 0:n], in0=up[bank_of[u]][:, 0:n],
                                                             scalar=bk[:, t:t + 1], in1=f32(kx[:, 2 * t, lo:lo + n]),
                                                             op0=ALU.add, op1=ALU.subtract)
                    else:
                        vp = (par + rel) % 2
                        ins = nc.vector.tensor_tensor(v_lo[:, vp, t], up[bank_of[u]][0:KR, :], f32(v_hi[:, vp, t]),
                                                      ALU.subtract)
                    ins.then_inc(unit_lo, 1)

                for u in order:
                    if u[3]:
                        unit(-1, u, 1)

                def normalise(b, k):
                    g = head(b, k)
                    dve.wait_ge(exp_done, g + 1)
                    nc.vector.reciprocal(row_inv[:, k % 2:k % 2 + 1], row_sum[:, k % 2:k % 2 + 1]).then_inc(inv_done, 1)
                    dve.wait_ge(inv_done, g + 1)
                    nc.vector.tensor_scalar(probs[:, k % 2, 0:NK], probs[:, k % 2, 0:NK], row_inv[:, k % 2:k % 2 + 1],
                                            None, ALU.mult).then_inc(p_done, 1)

                def program(b, par, last, half_b):
                    waiting = None
                    for s in slots(b, par, last):
                        if s[0] == "scores":
                            k = s[1]
                            g = head(b, k)
                            dve.wait_ge(s_done, g + 1)
                            nc.vector.tensor_reduce(neg_max[:, k % 2:k % 2 + 1], scores_at(k, last)[0:NQ, :, 0:KH],
                                                    mybir.AxisListType.XY, ALU.max, negate=True).then_inc(max_done, 1)
                            waiting = k
                            if k == 0 and isinstance(b, int) and b == 0:
                                normalise(b, k)
                                waiting = None
                        elif s[0] == "turn":
                            g = head(s[1], s[2])
                            dve.wait_ge(t_hi, g + 1)
                            h = s[2] % HP
                            nc.vector.tensor_tensor(pt_lo[:, :, h, :].rearrange("p (a j) q -> p a j q", a=2),
                                                    tp[0:KR, :, 0:3 * NQ].rearrange("p a (j q) -> p a j q", j=3),
                                                    f32(pt_hi[:, :, h, :]).rearrange("p (a j) q -> p a j q", a=2),
                                                    ALU.subtract).then_inc(t_lo, 1)
                            if waiting is not None:
                                normalise(b, waiting)
                                waiting = None
                        elif s[0] == "evacuate":
                            unit(s[1], s[3], s[2])
                        elif s[0] == "values":
                            _, vb, t = s
                            op = par if vb is b else 1 - par
                            dve.wait_ge(rest_done if BOTH else pv_done, group(vb, t) + 1)
                            if t == 0:
                                dve.wait_ge(o_stored[op], half_b * 16)
                            for j in range(HP):
                                rows = slice(j * HD, (j + 1) * HD)
                                here = slice(j * NQ, (j + 1) * NQ)
                                if BOTH:
                                    ins = nc.vector.tensor_tensor(o_t[rows, op, t, :], pv[rows, here], pv_rest[rows, here],
                                                                  ALU.add)
                                else:
                                    ins = nc.vector.tensor_scalar(o_t[rows, op, t, :], pv[rows, here], bv[rows, t:t + 1],
                                                                  None, ALU.add)
                            ins.then_inc(o_done, 1)

                batches(dve, program)


def output_stage(nc, tag, ident, x_rows, wo_t, bo, attended, wg, bg_cols, acc, table, logits_t, logits, gated, keep):
    x_all, xn, zero, gate, gates, stored = keep
    T = wo_t.shape[0] // P
    CG = 4
    NG = NB // CG
    with ExitStack() as ctx:
        st = Stage(nc, ctx, tag)
        ln = layernorm_buffers(st)
        stats, moments, veps, std, rstd, _ = ln
        bo_all = st.sb("bo", [NQ, D], F32)
        g_raw = st.sb("g_raw", [P, DC, P], F32)
        g_hi = st.sb("g_hi", [P, DC, P], F32R)
        g_lo = st.sb("g_lo", [P, DC, P], F32R)
        bg = st.sb("bg", [P, 1], F32)
        step = st.sem("step")
        x_in, w_in, b_in, o_in = st.sem("x_in"), st.sem("w_in"), st.sem("b_in"), [st.sem(f"o_in{i}") for i in range(2)]
        passed = st.sem("passed")
        with ExitStack() as inner:
            it = Stage(nc, inner, tag + "a")
            w_raw = it.sb("w_raw", [P, T, D], F32)
            w_hi = it.sb("w_hi", [P, T, D], F32R)
            w_lo = it.sb("w_lo", [P, T, D], F32R)
            o_raw = it.sb("o_raw", [P, 2, T, NQ], F32)
            o_hi = it.sb("o_hi", [P, 2, T, NQ], F32R)
            o_lo = it.sb("o_lo", [P, 2, T, NQ], F32R)
            yp = [it.ps(f"yp{i}", [P, D]) for i in range(2)]
            w_hi_done, w_lo_done, g_hi_done, g_lo_done = (it.sem(n) for n in ("w_hi_done", "w_lo_done", "g_hi_done", "g_lo_done"))
            o_hi_done, o_lo_done, x_biased = (it.sem(n) for n in ("o_hi_done", "o_lo_done", "x_biased"))
            stats_done = it.sem("stats_done")
            y_done, y_read = ([it.sem(f"{n}{i}") for i in range(2)] for n in ("y_done", "y_read"))
            with nc.Block() as block:
                @block.sync
                def _(sp):
                    sp.dma_start(w_raw[:], wo_t.rearrange("(t p) n -> p t n", p=P)).then_inc(w_in, 16)
                    sp.dma_start(bo_all[:], bo.partition_broadcast(NQ)).then_inc(b_in, 16)
                    sp.dma_start(g_raw[:], wg.rearrange("(c p) n -> p c n", p=P)).then_inc(b_in, 16)
                    sp.dma_start(bg[:], bg_cols).then_inc(b_in, 16)
                    sp.dma_start(x_all[:], x_rows.rearrange("(b p) d -> p b d", p=NQ)).then_inc(x_in, 16)
                    with sp.Fori(0, NB // 2) as i:
                        for par in range(2):
                            b = i * 2 + par
                            sp.wait_ge(o_lo_done, i * 2)
                            sp.dma_start(o_raw[:, par], attended[:, bass.ds(b, 1)].rearrange("p o t q -> p (o t) q")
                                         ).then_inc(o_in[par], 16)

                @block.gpsimd
                def _(pool):
                    wait_first(pool, x_in, 16, passed)
                    wait_first(pool, b_in, 48, passed)
                    for b in range(0, NB, 2):
                        nc.gpsimd.tensor_tensor(x_all[:, b:b + 2], x_all[:, b:b + 2],
                                                bo_all[:, :].unsqueeze(1).broadcast_to([NQ, 2, D]), ALU.add).then_inc(x_biased, 1)
                    nc.gpsimd.tensor_copy(g_hi[:], g_raw[:]).then_inc(g_hi_done, 1)
                    pool.wait_ge(g_hi_done, 1)
                    nc.gpsimd.tensor_tensor(g_lo[:], g_raw[:], f32(g_hi[:]), ALU.subtract).then_inc(g_lo_done, 1)
                    pool.wait_ge(g_lo_done, 1)

                @block.scalar
                def _(act):
                    act.wait_ge(w_in, 16)
                    nc.scalar.activation(w_hi[:], w_raw[:], ACT.Copy).then_inc(w_hi_done, 1)
                    with act.Fori(0, NB // 2) as i:
                        for par in range(2):
                            act.wait_ge(o_in[par], i * 16 + 16)
                            act.wait_ge(y_done[par], i)
                            nc.scalar.activation(o_hi[:, par], o_raw[:, par], ACT.Copy).then_inc(o_hi_done, 1)

                @block.vector
                def _(dve):
                    nc.vector.memset(zero[:], 0.0)
                    dve.wait_ge(w_hi_done, 1)
                    nc.vector.tensor_tensor(w_lo[:], w_raw[:], f32(w_hi[:]), ALU.subtract).then_inc(w_lo_done, 1)

                    def split(b, par):
                        dve.wait_ge(o_hi_done, b + 1)
                        nc.vector.tensor_tensor(o_lo[:, par], o_raw[:, par], f32(o_hi[:, par]),
                                                ALU.subtract).then_inc(o_lo_done, 1)

                    def add(i, par):
                        dve.wait_ge(y_done[par], i + 1)
                        cur = x_all[:, bass.ds(i * 2 + par, 1)].rearrange("p o d -> p (o d)")
                        nc.vector.tensor_tensor(cur, yp[par][0:NQ, :], cur, ALU.add).then_inc(y_read[par], 1)
                        dve.wait_ge(y_read[par], i + 1)
                        row_stats(nc, stats, x_all, i * 2 + par).then_inc(stats_done, 1)

                    split(0, 0)
                    split(1, 1)
                    with dve.Fori(0, NB // 2 - 1) as i:
                        dve.wait_ge(x_biased, i + 1)
                        add(i, 0)
                        split(i * 2 + 2, 0)
                        add(i, 1)
                        split(i * 2 + 3, 1)
                    dve.wait_ge(x_biased, NB // 2)
                    add(NB // 2 - 1, 0)
                    add(NB // 2 - 1, 1)
                    dve.wait_ge(stats_done, NB)

                @block.tensor
                def _(pe):
                    pe.wait_ge(w_hi_done, 1)
                    pe.wait_ge(w_lo_done, 1)
                    with pe.Fori(0, NB // 2) as i:
                        for par in range(2):
                            b = i * 2 + par
                            pe.wait_ge(o_lo_done, b + 1)
                            pe.wait_ge(y_read[par], i)
                            product(nc, yp[par][0:NQ, :], [
                                ((o_hi[:, par, t], o_lo[:, par, t]), (w_hi[:, t], w_lo[:, t])) for t in range(T)
                            ]).then_inc(y_done[par], 1)

        with ExitStack() as inner:
            it = Stage(nc, inner, tag + "b")
            xt_hi = it.sb("xt_hi", [P, DC, NT], F32R)
            xt_lo = it.sb("xt_lo", [P, DC, NT], F32R)
            xp = [it.ps(f"xp{i}", [P, DC, P]) for i in range(2)]
            lp = [it.ps(f"lp{i}", [P, CG * NQ]) for i in range(2)]
            tp = it.ps("tp", [P, NB, E])
            soft = it.sb("soft", [NQ, NB, E], F32)
            top = it.sb("top", [NQ, NB], F32)
            total = it.sb("total", [NQ, NB], F32)
            var_ready, std_ready = it.sem("var_ready"), it.sem("std_ready")
            xn_ready, xt_done, xt_hi_done, xt_lo_done = (it.sem(n) for n in ("xn_ready", "xt_done", "xt_hi_done", "xt_lo_done"))
            l_done, l_copied, lt_done, lt_copied = (it.sem(n) for n in ("l_done", "l_copied", "lt_done", "lt_copied"))
            shifted, gates_ready, rows_ready = it.sem("shifted"), it.sem("gates_ready"), it.sem("rows_ready")
            soft_ready = it.sem("soft_ready")
            with nc.Block() as block:
                @block.sync
                def _(sp):
                    rows = lambda t, w: t[0:NT, w].rearrange("(b p) d -> p b d", p=NQ)
                    sp.dma_start(rows(acc, slice(0, D)), x_all[:]).then_inc(stored, 16)
                    for r in range(SLOT_MAX // NQ):
                        at = slice(NT + r * NQ, NT + (r + 1) * NQ)
                        sp.dma_start(acc[at, :], zero[:, 0:D]).then_inc(stored, 16)
                        sp.dma_start(table[at, :], zero[:]).then_inc(stored, 16)
                    if not gated:
                        sp.wait_ge(rows_ready, 1)
                        sp.dma_start(rows(table, slice(0, D)), xn[:]).then_inc(stored, 16)

                @block.vector
                def _(dve):
                    chain = Chain(dve, step)
                    layernorm_scales(nc, dve, chain, ln, var_ready, std_ready)

                    def split_low(b):
                        dve.wait_ge(xt_hi_done, b + 1)
                        cols = slice(b * NQ, (b + 1) * NQ)
                        nc.vector.tensor_tensor(xt_lo[:, :, cols], xp[b % 2][:, :, 0:NQ], f32(xt_hi[:, :, cols]),
                                                ALU.subtract).then_inc(xt_lo_done, 1)

                    for b in range(NB):
                        nc.vector.tensor_scalar(xn[:, b, :], x_all[:, b, :], moments[:, b, 0:1], rstd[:, b:b + 1],
                                                ALU.subtract, ALU.mult).then_inc(xn_ready, 1)
                        if b:
                            split_low(b - 1)
                    split_low(NB - 1)
                    dve.wait_ge(xn_ready, NB)
                    nc.vector.memset(total[:], 0.0).then_inc(rows_ready, 1)
                    for g in range(NG):
                        dve.wait_ge(l_done, g + 1)
                        nc.vector.tensor_scalar(logits_t[:, g * CG * NQ:(g + 1) * CG * NQ], lp[g % 2][:], bg[:, 0:1], None,
                                                ALU.add).then_inc(l_copied, 1)
                    dve.wait_ge(lt_done, 1)
                    nc.vector.tensor_copy(logits[:], tp[0:NQ]).then_inc(lt_copied, 1)
                    if gated:
                        dve.wait_ge(lt_copied, 1)
                        chain.link(nc.vector.tensor_reduce(top[:], logits[:], AX_X, ALU.max))
                        nc.vector.tensor_tensor(soft[:], logits[:], top[:, :].unsqueeze(2).broadcast_to([NQ, NB, E]),
                                                ALU.subtract).then_inc(shifted, 1)
                        dve.wait_ge(soft_ready, 1)
                        chain.link(nc.vector.tensor_reduce(total[:], soft[:], AX_X, ALU.add))
                        chain.link(nc.vector.reciprocal(gate[:], total[:]))
                        nc.vector.tensor_copy(gates[:], gate[:, :].unsqueeze(2).broadcast_to([NQ, NB, E])).then_inc(gates_ready, 1)
                        dve.wait_ge(gates_ready, 1)

                @block.scalar
                def _(act):
                    act.wait_ge(var_ready, 1)
                    nc.scalar.activation(std[:], veps[:], ACT.Sqrt).then_inc(std_ready, 1)
                    for b in range(NB):
                        act.wait_ge(xt_done, b + 1)
                        nc.scalar.activation(xt_hi[:, :, b * NQ:(b + 1) * NQ], xp[b % 2][:, :, 0:NQ],
                                             ACT.Copy).then_inc(xt_hi_done, 1)
                    if gated:
                        act.wait_ge(shifted, 1)
                        nc.scalar.activation(soft[:], soft[:], ACT.Exp).then_inc(soft_ready, 1)
                    else:
                        act.wait_ge(lt_copied, 1)
                        nc.scalar.activation(gates[:], logits[:], ACT.Sigmoid).then_inc(gates_ready, 1)
                        act.wait_ge(gates_ready, 1)

                @block.tensor
                def _(pe):
                    for b in range(NB):
                        pe.wait_ge(xn_ready, b + 1)
                        if b >= 2:
                            pe.wait_ge(xt_lo_done, b - 1)
                        for c in range(DC):
                            last = nc.tensor.transpose(xp[b % 2][:, c, 0:NQ], xn[:, b, c * P:(c + 1) * P],
                                                       ident[0:NQ, 0:NQ])
                        last.then_inc(xt_done, 1)
                    for g in range(NG):
                        pe.wait_ge(xt_lo_done, CG * (g + 1))
                        if g >= 2:
                            pe.wait_ge(l_copied, g - 1)
                        cols = slice(g * CG * NQ, (g + 1) * CG * NQ)
                        product(nc, lp[g % 2][:], [((g_hi[:, c], g_lo[:, c]), (xt_hi[:, c, cols], xt_lo[:, c, cols]))
                                                   for c in range(DC)]).then_inc(l_done, 1)
                    pe.wait_ge(l_copied, NG)
                    for b in range(NB):
                        last = nc.tensor.transpose(tp[0:NQ, b], logits_t[0:E, b * NQ:(b + 1) * NQ], ident[0:E, 0:E])
                    last.then_inc(lt_done, 1)


def route_stage(nc, tag, ident, logits_t, logits, choose, slots, capacity, slot_rows, table, gated, keep):
    x_all, xn, zero, gate, gates, stored = keep
    NS = slots // NQ
    EXP_ONES = 0x7F800000
    with ExitStack() as ctx:
        st = Stage(nc, ctx, tag)
        tri = st.sb("tri", [NQ, NQ], BF16)
        ones = st.sb("ones", [NQ, NQ], BF16)
        slot_id = st.sb("slot_id", [NQ, NQ], F16)
        token = st.sb("token", [NQ, NB, 2], F16)
        dummy = st.sb("dummy", [NQ, NS], F32)
        chosen = st.sb("chosen", [NQ, NB, E], BF16)
        place = st.sb("place", [NQ, NB, E], F32)
        over = st.sb("over", [NQ, NB, E], F32)
        hundred = st.sb("hundred", [NQ, NB, E], F32)
        unit = st.sb("unit", [NQ, NB, E], F32)
        hot = st.sb("hot", [NQ, 2, NB, NQ], F16)
        marks = st.sb("marks", [NQ, NB, E, NS, 2], F16)
        count_ps = st.ps("count_ps", [P, NB, E])
        rows_ps = st.ps("rows_ps", [P, E * NS, 2])
        tmp = st.sb("tmp", [NQ, NB, E], F32)
        tmp2 = st.sb("tmp2", [NQ, E, NS], F32)
        tmp3 = st.sb("tmp3", [NQ, E, NS], F32)
        step, counted, chosen_ready = st.sem("step"), st.sem("counted"), st.sem("chosen_ready")
        hot_ready, hot_used = st.sem("hot_ready"), st.sem("hot_used")
        consts, zero_made, scaled = st.sem("consts"), st.sem("zero_made"), st.sem("scaled")
        if choose == "tokens":
            diff = st.sb("diff", [P, P], I32)
            same = st.sb("same", [P, P], BF16)
            lane = st.sb("lane", [P, 1], I32)
            lane_f = st.sb("lane_f", [P, 1], F32)
            part = st.sb("part", [P, 8], I32)
            prefix = st.sb("prefix", [P, 1], I32)
            cand = st.sb("cand", [P, 3], I32)
            cnt = st.sb("cnt", [P, 1], F32)
            enough = st.sb("enough", [P, 1], BF16)
            digit = st.sb("digit", [P, 2], I32)
            seen = st.sb("seen", [P, NT], BF16)
            cut = st.sb("cut", [P, 2 * E], F32)
            cut_tok = st.sb("cut_tok", [NQ, 2 * E], F32)
            ones_f = st.sb("ones_f", [E, NQ], F32)
            eq = st.sb("eq", [NQ, NB, E], BF16)
            gt = st.sb("gt", [NQ, NB, E], F32)
            sum_ps = st.ps("sum_ps", [P, 8])
            cut_ps = st.ps("cut_ps", [P, 2 * E])
            enough_ready, digit_ready, cut_ready, cut_done = (st.sem(n) for n in ("enough_ready", "digit_ready", "cut_ready", "cut_done"))
            eq_ready = st.sem("eq_ready")
        else:
            rank = st.sb("rank", [NQ, NB, E], F32)
            top = st.sb("top", [NQ, NB], F32)

        counts = 2 if choose == "tokens" else 1

        def running_count(pe, mask, done):
            nc.tensor.matmul(count_ps[0:NQ], tri[:], mask[:], start=True, stop=False)
            for b in range(NB - 1):
                rest = NB - 1 - b
                last = nc.tensor.matmul(count_ps[0:NQ, b + 1:NB, :], ones[:],
                                        mask[:, b:b + 1, :].broadcast_to([NQ, rest, E]),
                                        start=False, stop=(b == NB - 2))
            last.then_inc(done, 1)

        def search(dve, chain):
            chain.link(nc.vector.tensor_scalar(diff[:], diff[:], E - 1, None, ALU.bitwise_and))
            chain.link(nc.vector.tensor_scalar(same[:], diff[:], 0, None, ALU.is_equal))
            chain.link(nc.vector.memset(same[0:E, :], 0.0))
            chain.link(nc.vector.tensor_scalar(lane[:], lane[:], 3, None, ALU.logical_shift_right))
            chain.link(nc.vector.tensor_copy(lane_f[:], lane[:]))
            chain.link(nc.vector.tensor_scalar(lane_f[:], lane_f[:], float(E - 1), None, ALU.min))
            for j in range(8):
                ins = nc.vector.tensor_scalar(part[:, j:j + 1], lane[:], 28 - 4 * j, None, ALU.logical_shift_left)
            chain.step(ins)
            chain.link(nc.vector.memset(prefix[:], 0))

            def as_float():
                chain.link(nc.vector.tensor_scalar(cand[:, 1:2], cand[:, 0:1], 31, -1, ALU.arith_shift_right, ALU.bitwise_xor))
                chain.link(nc.vector.tensor_scalar(cand[:, 1:2], cand[:, 1:2], -2147483648, None, ALU.bitwise_or))
                chain.link(nc.vector.tensor_tensor(cand[:, 2:3], cand[:, 0:1], cand[:, 1:2], ALU.bitwise_xor))

            def finite():
                chain.link(nc.vector.tensor_scalar(cand[:, 0:1], cand[:, 2:3], EXP_ONES, None, ALU.bitwise_and))
                chain.link(nc.vector.tensor_scalar(cand[:, 0:1], cand[:, 0:1], float(EXP_ONES), -1.0, ALU.is_equal, ALU.mult))
                chain.link(nc.vector.tensor_scalar(cand[:, 1:2], cand[:, 0:1], 0x7FFFFF, None, ALU.bitwise_and))
                chain.link(nc.vector.tensor_scalar(cand[:, 0:1], cand[:, 0:1], 0x800000, None, ALU.bitwise_and))
                chain.link(nc.vector.tensor_tensor(cand[:, 2:3], cand[:, 2:3], cand[:, 1:2], ALU.bitwise_or))
                chain.link(nc.vector.tensor_tensor(cand[:, 2:3], cand[:, 2:3], cand[:, 0:1], ALU.bitwise_xor))

            for j in range(8):
                chain.link(nc.vector.tensor_tensor(cand[:, 0:1], prefix[:], part[:, j:j + 1], ALU.bitwise_or))
                as_float()
                if j < 3:
                    finite()
                chain.link(nc.vector.tensor_scalar(seen[:], logits_t[:], f32(cand[:, 2:3]), 0.0, ALU.is_ge, ALU.add,
                                                   accum_out=cnt[:]))
                nc.vector.tensor_scalar(enough[:], cnt[:], float(slots), None, ALU.is_ge).then_inc(enough_ready, 1)
                dve.wait_ge(digit_ready, j + 1)
                chain.link(nc.vector.tensor_copy(digit[:, 0:1], sum_ps[:, j:j + 1]))
                chain.link(nc.vector.tensor_scalar(digit[:, 1:2], digit[:, 0:1], 28 - 4 * j, None, ALU.logical_shift_left))
                chain.link(nc.vector.tensor_tensor(prefix[:], prefix[:], digit[:, 1:2], ALU.bitwise_or))
            chain.link(nc.vector.tensor_tensor(cand[:, 0:1], prefix[:], prefix[:], ALU.bitwise_or))
            as_float()
            finite()
            chain.link(nc.vector.tensor_scalar(seen[:], logits_t[:], f32(cand[:, 2:3]), 0.0, ALU.is_gt, ALU.add,
                                               accum_out=cnt[:]))
            chain.link(nc.vector.tensor_scalar(cnt[:], cnt[:], -1.0, float(slots), ALU.mult, ALU.add))
            chain.link(nc.vector.tensor_scalar(cut[0:E, 0:E], ident[0:E, 0:E], f32(cand[0:E, 2:3]), None, ALU.mult))
            chain.link(nc.vector.tensor_scalar(cut[0:E, E:2 * E], ident[0:E, 0:E], cnt[0:E], None, ALU.mult))
            nc.vector.memset(ones_f[:], 1.0).then_inc(cut_ready, 1)
            dve.wait_ge(cut_done, 1)
            chain.link(nc.vector.tensor_copy(cut_tok[:], cut_ps[0:NQ]))
            value = cut_tok[:, 0:E].unsqueeze(1).broadcast_to([NQ, NB, E])
            quota = cut_tok[:, E:2 * E].unsqueeze(1).broadcast_to([NQ, NB, E])
            nc.vector.tensor_tensor(eq[:], logits[:], value, ALU.is_equal).then_inc(eq_ready, 1)
            chain.link(nc.vector.tensor_tensor(gt[:], logits[:], value, ALU.is_gt))
            dve.wait_ge(counted, 1)
            chain.link(nc.vector.tensor_tensor(tmp[:], count_ps[0:NQ], quota, ALU.is_le))
            chain.link(nc.vector.tensor_tensor(tmp[:], tmp[:], eq[:], ALU.mult))
            nc.vector.tensor_tensor(chosen[:], tmp[:], gt[:], ALU.add).then_inc(chosen_ready, 1)

        with nc.Block() as block:
            @block.sync
            def _(sp):
                rows = lambda w: table[0:NT, w].rearrange("(b p) d -> p b d", p=NQ)
                if gated:
                    sp.wait_ge(scaled, NB)
                    sp.dma_start(rows(slice(0, D)), xn[:]).then_inc(stored, 16)
                with nc.allow_non_contiguous_dma(reason="eight gates at the end of each row"):
                    sp.dma_start(rows(slice(D, TABLE_W)), gates[:]).then_inc(stored, 16)
                sp.wait_ge(stored, 16 * (3 + 2 * (SLOT_MAX // NQ)))

            @block.scalar
            def _(act):
                if gated:
                    for b in range(NB):
                        nc.scalar.activation(xn[:, b], xn[:, b], ACT.Copy, scale=gate[:, b:b + 1]).then_inc(scaled, 1)

            @block.gpsimd
            def _(pool):
                nc.gpsimd.memset(tri[:], 1.0).then_inc(zero_made, 1)
                nc.gpsimd.memset(ones[:], 1.0).then_inc(consts, 1)
                pool.wait_ge(zero_made, 1)
                nc.gpsimd.affine_select(out=tri[:], in_=tri[:], compare_op=ALU.is_ge, fill=0.0, base=0,
                                        pattern=[[1, NQ]], channel_multiplier=-1).then_inc(consts, 1)
                nc.gpsimd.iota(slot_id[:], pattern=[[1, NQ]], base=1, channel_multiplier=0,
                               allow_small_or_imprecise_dtypes=True).then_inc(consts, 1)
                nc.gpsimd.iota(token[:, :, 0], pattern=[[NQ, NB]], base=0, channel_multiplier=1,
                               allow_small_or_imprecise_dtypes=True).then_inc(consts, 1)
                nc.gpsimd.memset(token[:, :, 1], 1.0).then_inc(consts, 1)
                nc.gpsimd.iota(dummy[:], pattern=[[NQ, NS]], base=NT, channel_multiplier=1,
                               allow_small_or_imprecise_dtypes=True).then_inc(consts, 1)
                if choose == "tokens":
                    nc.gpsimd.iota(diff[:], pattern=[[-1, P]], base=P, channel_multiplier=1).then_inc(consts, 1)
                    nc.gpsimd.iota(lane[:], pattern=[[0, 1]], base=0, channel_multiplier=1).then_inc(consts, 1)
                else:
                    nc.gpsimd.iota(rank[:], pattern=[[0, NB], [-1, E]], base=E, channel_multiplier=0,
                                   allow_small_or_imprecise_dtypes=True).then_inc(consts, 1)
            NCONST = 8 if choose == "tokens" else 7

            @block.vector
            def _(dve):
                chain = Chain(dve, step)
                dve.wait_ge(consts, NCONST)
                if choose == "tokens":
                    search(dve, chain)
                else:
                    chain.link(nc.vector.tensor_reduce(top[:], logits[:], AX_X, ALU.max))
                    chain.link(nc.vector.tensor_tensor(tmp[:], logits[:], top[:, :].unsqueeze(2).broadcast_to([NQ, NB, E]),
                                                       ALU.is_equal))
                    chain.link(nc.vector.tensor_tensor(tmp[:], tmp[:], rank[:], ALU.mult))
                    chain.link(nc.vector.tensor_reduce(top[:], tmp[:], AX_X, ALU.max))
                    nc.vector.tensor_tensor(chosen[:], rank[:], top[:, :].unsqueeze(2).broadcast_to([NQ, NB, E]),
                                            ALU.is_equal).then_inc(chosen_ready, 1)
                dve.wait_ge(chosen_ready, 1)
                dve.wait_ge(counted, counts)
                chain.link(nc.vector.tensor_tensor(place[:], count_ps[0:NQ], chosen[:], ALU.mult))
                if capacity is not None:
                    chain.link(nc.vector.scalar_tensor_tensor(out=place[:], in0=place[:], scalar=float(capacity),
                                                              in1=place[:], op0=ALU.is_lt, op1=ALU.mult))
                chain.link(nc.vector.tensor_scalar(hundred[:], place[:], float(NQ), None, ALU.is_gt))
                for s in range(2, NS):
                    chain.link(nc.vector.tensor_scalar(over[:], place[:], float(s * NQ), None, ALU.is_gt))
                    chain.link(nc.vector.tensor_tensor(hundred[:], hundred[:], over[:], ALU.add))
                chain.link(nc.vector.scalar_tensor_tensor(out=unit[:], in0=hundred[:], scalar=float(-NQ), in1=place[:],
                                                          op0=ALU.mult, op1=ALU.add))
                for s in range(NS):
                    ins = nc.vector.tensor_scalar(marks[:, :, :, s, 1], hundred[:], float(s), None, ALU.is_equal)
                chain.link(ins)
                number = token[:, :, 0:1].broadcast_to([NQ, NB, E])
                for s in range(NS):
                    ins = nc.vector.tensor_tensor(marks[:, :, :, s, 0], marks[:, :, :, s, 1], number, ALU.mult)
                chain.link(ins)
                for e in range(E):
                    if e >= 2:
                        dve.wait_ge(hot_used, e - 1)
                    for b in range(NB):
                        ins = nc.vector.tensor_scalar(hot[:, e % 2, b], slot_id[:], unit[:, b, e:e + 1], None, ALU.is_equal)
                    ins.then_inc(hot_ready, 1)
                dve.wait_ge(hot_used, E)
                ps = rows_ps[0:NQ].rearrange("p (e s) c -> p e s c", e=E)
                dm = dummy[:, :].unsqueeze(1).broadcast_to([NQ, E, NS])
                chain.link(nc.vector.tensor_tensor(tmp2[:], ps[:, :, :, 1], dm, ALU.mult))
                chain.link(nc.vector.tensor_tensor(tmp3[:], dm, tmp2[:], ALU.subtract))
                chain.link(nc.vector.tensor_tensor(tmp2[:], ps[:, :, :, 0], tmp3[:], ALU.add))
                chain.link(nc.vector.tensor_copy(slot_rows[:, 0:E * NS].rearrange("p (e s) -> p e s", e=E), tmp2[:]))
                chain.link(nc.vector.tensor_copy(slot_rows[:, E * NS:(E + 1) * NS], tmp2[:, 0, :]))

            @block.tensor
            def _(pe):
                pe.wait_ge(consts, NCONST)
                if choose == "tokens":
                    for j in range(8):
                        pe.wait_ge(enough_ready, j + 1)
                        nc.tensor.matmul(sum_ps[:, j:j + 1], same[:], enough[:], start=True, stop=True).then_inc(digit_ready, 1)
                    pe.wait_ge(cut_ready, 1)
                    nc.tensor.matmul(cut_ps[0:NQ], ones_f[:], cut[0:E], start=True, stop=True).then_inc(cut_done, 1)
                    pe.wait_ge(eq_ready, 1)
                    running_count(pe, eq, counted)
                pe.wait_ge(chosen_ready, 1)
                running_count(pe, chosen, counted)
                for e in range(E):
                    pe.wait_ge(hot_ready, e + 1)
                    for b in range(NB):
                        last = nc.tensor.matmul(rows_ps[0:NQ, e * NS:(e + 1) * NS, :], hot[:, e % 2, b], marks[:, b, e],
                                                start=(b == 0), stop=(b == NB - 1))
                    last.then_inc(hot_used, 1)


def ffn_stage(nc, tag, ident, table, acc, slot_rows, w1, b1_cols, w2, b2, slots, act_func):
    NS = slots // NQ
    FF = w1.shape[2]
    FQ = 4
    NQD = FF // (FQ * P)
    FT = FQ * NQD
    with ExitStack() as ctx:
        st = Stage(nc, ctx, tag)
        w1_raw = st.sb("w1_raw", [P, 2, DC, FQ * P], F32)
        w2_raw = st.sb("w2_raw", [P, 2, FQ, D], F32)
        w1_hi, w1_lo = st.sb("w1_hi", [P, 2, DC, FQ * P], F32R), st.sb("w1_lo", [P, 2, DC, FQ * P], F32R)
        w2_hi, w2_lo = st.sb("w2_hi", [P, 2, FQ, D], F32R), st.sb("w2_lo", [P, 2, FQ, D], F32R)
        b1 = st.sb("b1", [P, E * FT], F32)
        b2_all = st.sb("b2", [NQ, 2, D], F32)
        rows_from = st.sb("rows_from", [NQ, 2, NS], U32)
        rows_to = st.sb("rows_to", [NQ, 2, NS], U32)
        xg = st.sb("xg", [NQ, 2, NS, TABLE_W], F32)
        xe_hi = st.sb("xe_hi", [P, 2, DC, slots], F32R)
        xe_lo = st.sb("xe_lo", [P, 2, DC, slots], F32R)
        h_val = st.sb("h_val", [P, 2, slots], F32)
        h_hi = st.sb("h_hi", [P, 2, slots], F32R)
        h_lo = st.sb("h_lo", [P, 2, slots], F32R)
        y_val = st.sb("y_val", [NQ, NS, D], F32)
        yp = [st.ps(f"yp{s}", [P, D]) for s in range(NS)]
        hp = [st.ps(f"hp{i}", [P, slots]) for i in range(2)]
        xp = [st.ps(f"xp{i}", [P, DC, P]) for i in range(2)]

        w_in = [st.sem(f"w_in{i}") for i in range(2)]
        b_in, b2_in = st.sem("b_in"), [st.sem(f"b2_in{i}") for i in range(2)]
        w1_hi_d, w1_lo_d, w2_hi_d, w2_lo_d = (st.sem(n) for n in ("w1_hi_d", "w1_lo_d", "w2_hi_d", "w2_lo_d"))
        rows_to_set = st.sem("rows_to_set")
        rows_set, gathered = st.sem("rows_set"), [st.sem(f"gathered{i}") for i in range(2)]
        x_turned, x_hi, x_lo = st.sem("x_turned"), st.sem("x_hi"), st.sem("x_lo")
        h_done, h_val_d, h_hi_d, h_lo_d = (st.sem(n) for n in ("h_done", "h_val_d", "h_hi_d", "h_lo_d"))
        y_done, y_biased, y_ready = st.sem("y_done"), st.sem("y_biased"), st.sem("y_ready")
        scattered, passed = st.sem("scattered"), st.sem("passed")

        def experts(eng, program):
            with eng.Fori(0, E // 2 - 1) as i:
                for ep in range(2):
                    program(i * 2 + ep, ep, i, False)
            for ep in range(2):
                program(E - 2 + ep, ep, E // 2 - 1, True)

        def ahead(ep, last):
            return not (last and ep == 1)

        with nc.Block() as block:
            @block.sync
            def _(sp):
                def load(i, u):
                    e, q, par = i * 2 + u // NQD, u % NQD, u % 2
                    cols = slice(q * FQ * P, (q + 1) * FQ * P)
                    sp.dma_start(w1_raw[:, par], w1[bass.ds(e, 1), :, cols].rearrange("o (c p) n -> p (o c) n", p=P)
                                 ).then_inc(w_in[par], 16)
                    sp.dma_start(w2_raw[:, par], w2[bass.ds(e, 1), cols, :].rearrange("o (c p) n -> p (o c) n", p=P)
                                 ).then_inc(w_in[par], 16)

                sp.dma_start(b1[:], b1_cols).then_inc(b_in, 16)
                load(0, 0)
                load(0, 1)

                def program(e, ep, i, last):
                    for q in range(NQD):
                        u = ep * NQD + q
                        if not last or u + 2 < 2 * NQD:
                            sp.wait_ge(w1_lo_d, e * NQD + q + 1)
                            sp.wait_ge(w2_lo_d, e * NQD + q + 1)
                            load(i, u + 2)
                        if q == 0:
                            sp.wait_ge(y_biased, (i * 2) * NS)
                            sp.dma_start(b2_all[:, ep], b2[bass.ds(e, 1), :].rearrange("o d -> (o d)").partition_broadcast(NQ)
                                         ).then_inc(b2_in[ep], 16)

                experts(sp, program)

            @block.gpsimd
            def _(pool):
                def gather(e, par):
                    nc.gpsimd.tensor_copy(rows_from[:, par], slot_rows[:, bass.ds(e * NS, NS)]).then_inc(rows_set, 1)
                    wait_first(pool, rows_set, e + 1, passed)
                    for s in range(NS):
                        nc.gpsimd.indirect_dma_start(
                            out=xg[:, par, s], out_offset=None, in_=table,
                            in_offset=bass.IndirectOffsetOnAxis(ap=rows_from[:, par, s:s + 1], axis=0)
                        ).then_inc(gathered[par], 16)

                def w2_low(n, par):
                    pool.wait_ge(w2_hi_d, n + 1)
                    nc.gpsimd.tensor_tensor(w2_lo[:, par], w2_raw[:, par], f32(w2_hi[:, par]), ALU.subtract).then_inc(w2_lo_d, 1)

                gather(0, 0)
                w2_low(0, 0)

                def program(e, ep, i, last):
                    for q in range(NQD):
                        if q == 0 and ahead(ep, last):
                            gather(e + 1, 1 - ep)
                        if q < NQD - 1 or ahead(ep, last):
                            w2_low(e * NQD + q + 1, (ep * NQD + q + 1) % 2)
                    wait_first(pool, scattered, e * (16 * NS), passed)
                    nc.gpsimd.tensor_copy(rows_to[:, ep], slot_rows[:, bass.ds(e * NS, NS)]).then_inc(rows_to_set, 1)
                    wait_first(pool, rows_to_set, e + 1, passed)
                    for s in range(NS):
                        wait_first(pool, y_ready, e * NS + s + 1, passed)
                        nc.gpsimd.indirect_dma_start(
                            out=acc, out_offset=bass.IndirectOffsetOnAxis(ap=rows_to[:, ep, s:s + 1], axis=0),
                            in_=y_val[:, s], in_offset=None, compute_op=ALU.add).then_inc(scattered, 16)

                experts(pool, program)
                wait_first(pool, scattered, E * (16 * NS), passed)

            @block.scalar
            def _(act):
                def x_high(e, par):
                    for s in range(NS):
                        act.wait_ge(x_turned, e * NS + s + 1)
                        nc.scalar.activation(xe_hi[:, par, :, s * NQ:(s + 1) * NQ], xp[s % 2][:, :, 0:NQ],
                                             ACT.Copy).then_inc(x_hi, 1)

                def w_high(par, uses):
                    act.wait_ge(w_in[par], uses * 32)
                    nc.scalar.activation(w1_hi[:, par], w1_raw[:, par], ACT.Copy).then_inc(w1_hi_d, 1)
                    nc.scalar.activation(w2_hi[:, par], w2_raw[:, par], ACT.Copy).then_inc(w2_hi_d, 1)

                w_high(0, 1)
                x_high(0, 0)
                act.wait_ge(b_in, 16)

                def program(e, ep, i, last):
                    for q in range(NQD):
                        u = ep * NQD + q
                        for f in range(FQ):
                            m = (e * NQD + q) * FQ + f
                            act.wait_ge(h_done, m + 1)
                            nc.scalar.activation(h_val[:, f % 2], hp[f % 2][:], act_func,
                                                 bias=b1[:, bass.ds(m, 1)]).then_inc(h_val_d, 1)
                            if f == 1 and (q < NQD - 1 or ahead(ep, last)):
                                w_high((u + 1) % 2, i * NQD + (u + 1) // 2 + 1)
                        if q == NQD // 2 and ahead(ep, last):
                            x_high(e + 1, 1 - ep)

                experts(act, program)

            @block.vector
            def _(dve):
                def x_low(e, par):
                    for s in range(NS):
                        dve.wait_ge(x_hi, e * NS + s + 1)
                        cols = slice(s * NQ, (s + 1) * NQ)
                        nc.vector.tensor_tensor(xe_lo[:, par, :, cols], xp[s % 2][:, :, 0:NQ], f32(xe_hi[:, par, :, cols]),
                                                ALU.subtract).then_inc(x_lo, 1)

                def w1_low(n, par):
                    dve.wait_ge(w1_hi_d, n + 1)
                    nc.vector.tensor_tensor(w1_lo[:, par], w1_raw[:, par], f32(w1_hi[:, par]), ALU.subtract).then_inc(w1_lo_d, 1)

                w1_low(0, 0)
                x_low(0, 0)

                def program(e, ep, i, last):
                    for q in range(NQD):
                        for f in range(FQ):
                            m = (e * NQD + q) * FQ + f
                            dve.wait_ge(h_val_d, m + 1)
                            nc.vector.tensor_copy(h_hi[:, f % 2], h_val[:, f % 2]).then_inc(h_hi_d, 1)
                            dve.wait_ge(h_hi_d, m + 1)
                            nc.vector.tensor_tensor(h_lo[:, f % 2], h_val[:, f % 2], f32(h_hi[:, f % 2]),
                                                    ALU.subtract).then_inc(h_lo_d, 1)
                            if f == 1 and (q < NQD - 1 or ahead(ep, last)):
                                w1_low(e * NQD + q + 1, (ep * NQD + q + 1) % 2)
                        if q == NQD // 2 and ahead(ep, last):
                            x_low(e + 1, 1 - ep)
                    dve.wait_ge(b2_in[ep], i * 16 + 16)
                    dve.wait_ge(scattered, e * (16 * NS))
                    for s in range(NS):
                        dve.wait_ge(y_done, e * NS + s + 1)
                        nc.vector.tensor_tensor(y_val[:, s], yp[s][0:NQ, :], b2_all[:, ep], ALU.add).then_inc(y_biased, 1)
                    for s in range(NS):
                        dve.wait_ge(y_biased, e * NS + s + 1)
                        gate = xg[:, ep, s, bass.ds(e + D, 1)]
                        nc.vector.tensor_scalar(y_val[:, s], y_val[:, s], gate, None, ALU.mult).then_inc(y_ready, 1)

                experts(dve, program)

            @block.tensor
            def _(pe):
                def turn(e, par, gathers):
                    pe.wait_ge(gathered[par], gathers * (16 * NS))
                    for s in range(NS):
                        pe.wait_ge(x_lo, e * NS + max(s - 1, 0))
                        for c in range(DC):
                            last = nc.tensor.transpose(xp[s % 2][:, c, 0:NQ], xg[:, par, s, c * P:(c + 1) * P],
                                                       ident[0:NQ, 0:NQ])
                        last.then_inc(x_turned, 1)

                turn(0, 0, 1)

                def program(e, ep, i, last):
                    def second(q, f):
                        m = (e * NQD + q) * FQ + f
                        par = (ep * NQD + q) % 2
                        first, final = q == 0 and f == 0, q == NQD - 1 and f == FQ - 1
                        if f == 0:
                            pe.wait_ge(w2_lo_d, e * NQD + q + 1)
                        pe.wait_ge(h_lo_d, m + 1)
                        for s in range(NS):
                            if first:
                                pe.wait_ge(y_biased, e * NS)
                            rows = slice(s * NQ, (s + 1) * NQ)
                            ops = three_passes((h_hi[:, f % 2, rows], h_lo[:, f % 2, rows]), (w2_hi[:, par, f], w2_lo[:, par, f]))
                            for k, (w, mv) in enumerate(ops):
                                mm = nc.tensor.matmul(yp[s][0:NQ, :], w, mv, start=(first and k == 0), stop=(final and k == 2))
                            if final:
                                mm.then_inc(y_done, 1)

                    before = None
                    pe.wait_ge(x_lo, e * NS + NS)
                    for q in range(NQD):
                        par = (ep * NQD + q) % 2
                        pe.wait_ge(w1_lo_d, e * NQD + q + 1)
                        for f in range(FQ):
                            cols = slice(f * P, (f + 1) * P)
                            product(nc, hp[f % 2][:], [
                                ((w1_hi[:, par, c, cols], w1_lo[:, par, c, cols]), (xe_hi[:, ep, c], xe_lo[:, ep, c]))
                                for c in range(DC)]).then_inc(h_done, 1)
                            if before is not None:
                                second(*before)
                            before = (q, f)
                        if q == NQD // 2 and ahead(ep, last):
                            turn(e + 1, 1 - ep, i + 1 + ep)
                    second(*before)

                experts(pe, program)


def two_layers_kernel(nc, a, out):
    scratch = lambda name, shape, dt=F32: nc.dram_tensor(name, shape, dt).ap()
    with ExitStack() as ctx:
        ident = ctx.enter_context(nc.sbuf_tensor("ident", [P, P], F32))
        setup_stage(nc, ident)
        x_rows = a["x"].rearrange("b q d -> (b q) d")
        layers = [
            dict(n=0, inner=1024, heads=16, rows=x_rows, slots=400, choose="tokens", capacity=None, func=ACT.Gelu, gated=False),
            dict(n=1, inner=512, heads=16, slots=200, choose="expert", capacity=NT // E, func=ACT.Relu, gated=True),
        ]
        for layer in layers:
            n = layer["n"]
            T = layer["inner"] // P
            HP = P // (layer["inner"] // layer["heads"])
            g = lambda name: a[f"L{n}_{name}"]
            rows = layer["rows"] if n == 0 else layers[0]["acc"][0:NT, :]
            queries = scratch(f"queries{n}", (P, NB, T, 2, NQ))
            attended = scratch(f"attended{n}", (P, NB, T, NQ))
            acc = layer["acc"] = out if n == 1 else scratch(f"acc{n}", (ROWS, D))
            table = scratch(f"table{n}", (ROWS, TABLE_W))
            hd = layer["inner"] // layer["heads"]
            query_stage(nc, f"q{n}", ident, rows, g("wq"), g("bq"), float(np.float32(hd) ** np.float32(-0.5)), queries)
            for h in range(T // TT):
                cols = slice(h * TW, (h + 1) * TW)
                tiles = slice(h * TT, (h + 1) * TT)
                attention_pass(nc, f"a{n}{h}", ident, h * TT, HP, a["ctx_t"], g("wk")[:, cols], g("wv")[:, cols],
                               g("bk")[:, tiles], g("bv")[:, tiles], queries, attended)
            with ExitStack() as mid:
                slot_rows = mid.enter_context(nc.sbuf_tensor(f"slot_rows{n}", [NQ, (E + 1) * (layer["slots"] // NQ)], U32))
                with ExitStack() as short:
                    hold = Stage(nc, short, f"k{n}")
                    keep = (hold.sb("x", [NQ, NB, D], F32), hold.sb("xn", [NQ, NB, D], F32),
                            hold.sb("zero", [NQ, TABLE_W], F32), hold.sb("gate", [NQ, NB], F32),
                            hold.sb("gates", [NQ, NB, E], F32), hold.sem("stored"))
                    logits_t = short.enter_context(nc.sbuf_tensor(f"logits_t{n}", [P, NT], F32))
                    logits = short.enter_context(nc.sbuf_tensor(f"logits{n}", [NQ, NB, E], F32))
                    output_stage(nc, f"o{n}", ident, rows, g("wo"), g("bo"), attended, g("wg"), g("bg"), acc, table,
                                 logits_t, logits, layer["gated"], keep)
                    route_stage(nc, f"r{n}", ident, logits_t, logits, layer["choose"], layer["slots"],
                                layer["capacity"], slot_rows, table, layer["gated"], keep)
                ffn_stage(nc, f"f{n}", ident, table, acc, slot_rows, g("w1"), g("b1"), g("w2"), g("b2"),
                          layer["slots"], layer["func"])


def kernel(**inputs):
    import concourse.bacc as _bacc
    from concourse import mybir as _mybir
    from concourse.bass_utils import run_bass_kernel_spmd as _run

    i = {k: np.asarray(v) for k, v in inputs.items()}
    cols = lambda b: b.reshape(-1, P).T
    hidden = lambda b: b.reshape(E, -1, P).transpose(2, 0, 1).reshape(P, -1)
    repeat = lambda w: np.tile(w, (1, REP))
    ctx_t = i["ctx_1024"].transpose(0, 2, 1)
    laid = {
        "x": i["x"],
        "ctx_t": np.concatenate([ctx_t, np.zeros((NB, D, NKP - NK), ctx_t.dtype)], axis=2),
        "L0_wq": i["L0_xattn_Wq"].T, "L0_bq": cols(i["L0_xattn_bq"]),
        "L0_wk": i["L0_xattn_Wk"].T, "L0_bk": cols(i["L0_xattn_bk"]),
        "L0_wv": i["L0_xattn_Wv"].T, "L0_bv": cols(i["L0_xattn_bv"]),
        "L0_wo": i["L0_xattn_Wo"].T, "L0_bo": i["L0_xattn_bo"],
        "L0_wg": repeat(i["L0_ffn_Wg"]), "L0_bg": np.zeros((P, 1), np.float32),
        "L0_w1": i["L0_ffn_W1"], "L0_b1": hidden(i["L0_ffn_b1"]), "L0_w2": i["L0_ffn_W2"], "L0_b2": i["L0_ffn_b2"],
        "L1_wq": i["L1_xattn_Wq"], "L1_bq": cols(i["L1_xattn_bq"]),
        "L1_wk": i["L1_xattn_Wkv"][:, 0:D], "L1_bk": cols(i["L1_xattn_bkv"][0:D]),
        "L1_wv": i["L1_xattn_Wkv"][:, D:2 * D], "L1_bv": cols(i["L1_xattn_bkv"][D:2 * D]),
        "L1_wo": i["L1_xattn_Wproj"], "L1_bo": i["L1_xattn_bproj"],
        "L1_wg": repeat(i["L1_ffn_Wr"]), "L1_bg": np.tile(i["L1_ffn_br"], REP).reshape(P, 1),
        "L1_w1": i["L1_ffn_W1"], "L1_b1": hidden(i["L1_ffn_b1"]), "L1_w2": i["L1_ffn_W2"], "L1_b2": i["L1_ffn_b2"],
    }
    nc = _bacc.Bacc("TRN2", target_bir_lowering=False, num_devices=1)
    arrays, args = {}, {}
    for name, value in laid.items():
        arrays[f"in_{name}"] = value = np.ascontiguousarray(value)
        args[name] = nc.dram_tensor(f"in_{name}", value.shape, _mybir.dt.from_np(value.dtype), kind="ExternalInput").ap()
    out = nc.dram_tensor("out", (ROWS, D), F32, kind="ExternalOutput").ap()
    two_layers_kernel(nc, args, out)
    r = _run(nc, [arrays], core_ids=[0])
    return r.results[0]["out"][0:NT].reshape(NB, NQ, D)
```
